# Optimizing a Trainium2 kernel written in Bass

```python
import numpy as np
import jax
import jax.numpy as jnp

def _softmax(x, axis=-1):
    return jax.nn.softmax(x, axis=axis)
def _gelu(x):
    return jax.nn.gelu(x, approximate=True)
def _silu(x):
    return jax.nn.silu(x)
def _sigmoid(x):
    return jax.nn.sigmoid(x)
def _layernorm(x, axis=-1, eps=1e-5):
    m = jnp.mean(x, axis=axis, keepdims=True)
    v = jnp.var(x, axis=axis, keepdims=True)
    return (x - m) / jnp.sqrt(v + eps)
def _scatter_add(tgt, idx, src, axis=0):
    return tgt.at[idx].add(src)
def _segment_sum(src, seg, n):
    return jax.ops.segment_sum(src, seg, n)

kernel_name = 'mk_conv_seq_d2_conv_nchw64_3b42f4'

def setup_inputs(seed: int = 0):
    np.random.seed(seed)
    _w = jnp.asarray
    def _rec_inputs():
        import jax
        import jax.numpy as jnp
        _gk = jax.random.key(seed)
        x = -0.0002091 + 1 * jax.random.normal(jax.random.fold_in(_gk, 1), (32, 64, 112, 112), jnp.float32)
        return x
    x = _rec_inputs()
    def _L0_conv_setup():
        import jax, jax.numpy as jnp
        import numpy as np
        BN_EPS = 1e-05

        def _binary_activation(x):
            s = jnp.sign(x)
            o1 = jnp.where(x < -1.0, -1.0, x * x + 2.0 * x)
            o2 = jnp.where(x < 0.0, o1, -x * x + 2.0 * x)
            o3 = jnp.where(x < 1.0, o2, 1.0)
            return jax.lax.stop_gradient(s - o3) + o3

        def _binarize_weights(w):
            sgn = 2.0 * (w > 0.0).astype(w.dtype) - 1.0
            wb = jax.lax.stop_gradient(sgn - w) + w
            scale = jax.lax.stop_gradient(jnp.mean(jnp.abs(w), axis=(1, 2, 3), keepdims=True))
            return scale * wb
        key = jax.random.key(seed)
        k1, k2, k3 = jax.random.split(key, 3)
        C = 64
        x = jax.random.normal(k1, (32, C, 112, 112), dtype=jnp.float32)
        w = jax.random.uniform(k2, (C, C, 3, 3), dtype=jnp.float32) * 0.001
        return {'x': x, 'b0': jnp.zeros((1, C, 1, 1), jnp.float32), 'w': w, 'gamma': jnp.ones((C,), jnp.float32), 'beta': jnp.zeros((C,), jnp.float32), 'b1': jnp.zeros((1, C, 1, 1), jnp.float32), 'alpha': jnp.full((C,), 0.25, jnp.float32), 'b2': jnp.zeros((1, C, 1, 1), jnp.float32)}
    _L0_conv_all = _L0_conv_setup()
    _L0_conv_in = {k: v for k, v in _L0_conv_all.items() if k in ('b0', 'w', 'gamma', 'beta', 'b1', 'alpha', 'b2', )}
    del _L0_conv_all

    def _L1_conv_setup():
        import jax, jax.numpy as jnp
        import numpy as np
        K = 3
        TAPS = K * K
        STD = float(np.sqrt(2.0)) / K

        def filter_norm(f, axis):
            m = jnp.mean(f, axis=axis, keepdims=True)
            sd = jnp.std(f, axis=axis, keepdims=True, ddof=1)
            return (f - m) / (sd + 1e-10) * STD

        def block_forward(x, sw, sb, cw1, cb1, cw2, cb2, w2, b2):
            B, C, H, W = x.shape
            s = jnp.einsum('bchw,tc->bthw', x, sw) + sb[None, :, None, None]
            s = filter_norm(s, axis=1)
            g = x.mean(axis=(2, 3))
            h1 = jax.nn.relu(g @ cw1.T + cb1)
            cf = (h1 @ cw2.T + cb2).reshape(B, C, TAPS)
            cf = filter_norm(cf, axis=2)
            xp = jnp.pad(x, ((0, 0), (0, 0), (1, 1), (1, 1)))
            out = jnp.zeros_like(x)
            for idx in range(TAPS):
                i, j = (idx // K, idx % K)
                out = out + xp[:, :, i:i + H, j:j + W] * s[:, idx:idx + 1] * cf[:, :, idx, None, None]
            a = jnp.where(out >= 0, out, 0.1 * out)
            y = jax.lax.conv_general_dilated(a, w2, (1, 1), ((0, 0), (4, 4)), dimension_numbers=('NCHW', 'OIHW', 'NCHW'))
            y = y + b2[None, :, None, None]
            return x + y
        key = jax.random.key(seed)
        ks = jax.random.split(key, 9)
        B, C, H, W = (4, 64, 192, 192)
        mid = int(C * 0.2)
        f = lambda k, shape, s: jax.random.normal(k, shape, jnp.float32) * s
        return {'x': f(ks[0], (B, C, H, W), 1.0), 'sw': f(ks[1], (TAPS, C), 0.05), 'sb': f(ks[2], (TAPS,), 0.05), 'cw1': f(ks[3], (mid, C), 0.05), 'cb1': f(ks[4], (mid,), 0.05), 'cw2': f(ks[5], (C * TAPS, mid), 0.05), 'cb2': f(ks[6], (C * TAPS,), 0.05), 'w2': f(ks[7], (C, C, 1, 9), 0.05), 'b2': f(ks[8], (C,), 0.05)}
    _L1_conv_all = _L1_conv_setup()
    _L1_conv_in = {k: v for k, v in _L1_conv_all.items() if k in ('sw', 'sb', 'cw1', 'cb1', 'cw2', 'cb2', 'w2', 'b2', )}
    del _L1_conv_all

    return {
        "x": x,
        "L0_conv_b0": _L0_conv_in["b0"],
        "L0_conv_w": _L0_conv_in["w"],
        "L0_conv_gamma": _L0_conv_in["gamma"],
        "L0_conv_beta": _L0_conv_in["beta"],
        "L0_conv_b1": _L0_conv_in["b1"],
        "L0_conv_alpha": _L0_conv_in["alpha"],
        "L0_conv_b2": _L0_conv_in["b2"],
        "L1_conv_sw": _L1_conv_in["sw"],
        "L1_conv_sb": _L1_conv_in["sb"],
        "L1_conv_cw1": _L1_conv_in["cw1"],
        "L1_conv_cb1": _L1_conv_in["cb1"],
        "L1_conv_cw2": _L1_conv_in["cw2"],
        "L1_conv_cb2": _L1_conv_in["cb2"],
        "L1_conv_w2": _L1_conv_in["w2"],
        "L1_conv_b2": _L1_conv_in["b2"],
    }

def reference(x, L0_conv_b0, L0_conv_w, L0_conv_gamma, L0_conv_beta, L0_conv_b1, L0_conv_alpha, L0_conv_b2, L1_conv_sw, L1_conv_sb, L1_conv_cw1, L1_conv_cb1, L1_conv_cw2, L1_conv_cb2, L1_conv_w2, L1_conv_b2):
    import jax
    import jax.numpy as jnp
    def _L0_conv_ref(x, b0, w, gamma, beta, b1, alpha, b2):
        import jax, jax.numpy as jnp
        import numpy as np
        BN_EPS = 1e-05

        def _binary_activation(x):
            s = jnp.sign(x)
            o1 = jnp.where(x < -1.0, -1.0, x * x + 2.0 * x)
            o2 = jnp.where(x < 0.0, o1, -x * x + 2.0 * x)
            o3 = jnp.where(x < 1.0, o2, 1.0)
            return jax.lax.stop_gradient(s - o3) + o3

        def _binarize_weights(w):
            sgn = 2.0 * (w > 0.0).astype(w.dtype) - 1.0
            wb = jax.lax.stop_gradient(sgn - w) + w
            scale = jax.lax.stop_gradient(jnp.mean(jnp.abs(w), axis=(1, 2, 3), keepdims=True))
            return scale * wb
        residual = x
        out = x + b0
        out = _binary_activation(out)
        bw = _binarize_weights(w)
        out = jax.lax.conv_general_dilated(out, bw, window_strides=(1, 1), padding=[(1, 1), (1, 1)], dimension_numbers=('NCHW', 'OIHW', 'NCHW'))
        mu = jnp.mean(out, axis=(0, 2, 3), keepdims=True)
        var = jnp.var(out, axis=(0, 2, 3), keepdims=True)
        g = gamma.reshape(1, -1, 1, 1)
        b = beta.reshape(1, -1, 1, 1)
        out = (out - mu) * jax.lax.rsqrt(var + BN_EPS) * g + b
        out = out + residual
        out = out + b1
        a = alpha.reshape(1, -1, 1, 1)
        out = jnp.where(out > 0, out, a * out)
        out = out + b2
        return out

    def _L1_conv_ref(x, sw, sb, cw1, cb1, cw2, cb2, w2, b2):
        import jax, jax.numpy as jnp
        import numpy as np
        K = 3
        TAPS = K * K
        STD = float(np.sqrt(2.0)) / K

        def filter_norm(f, axis):
            m = jnp.mean(f, axis=axis, keepdims=True)
            sd = jnp.std(f, axis=axis, keepdims=True, ddof=1)
            return (f - m) / (sd + 1e-10) * STD

        def block_forward(x, sw, sb, cw1, cb1, cw2, cb2, w2, b2):
            B, C, H, W = x.shape
            s = jnp.einsum('bchw,tc->bthw', x, sw) + sb[None, :, None, None]
            s = filter_norm(s, axis=1)
            g = x.mean(axis=(2, 3))
            h1 = jax.nn.relu(g @ cw1.T + cb1)
            cf = (h1 @ cw2.T + cb2).reshape(B, C, TAPS)
            cf = filter_norm(cf, axis=2)
            xp = jnp.pad(x, ((0, 0), (0, 0), (1, 1), (1, 1)))
            out = jnp.zeros_like(x)
            for idx in range(TAPS):
                i, j = (idx // K, idx % K)
                out = out + xp[:, :, i:i + H, j:j + W] * s[:, idx:idx + 1] * cf[:, :, idx, None, None]
            a = jnp.where(out >= 0, out, 0.1 * out)
            y = jax.lax.conv_general_dilated(a, w2, (1, 1), ((0, 0), (4, 4)), dimension_numbers=('NCHW', 'OIHW', 'NCHW'))
            y = y + b2[None, :, None, None]
            return x + y
        return block_forward(x, sw, sb, cw1, cb1, cw2, cb2, w2, b2)

    def _gn(v, G=32, eps=1e-5):
        B_, C_, H_, W_ = v.shape
        g = v.reshape(B_, G, C_ // G, H_, W_)
        m = jnp.mean(g, axis=(2, 3, 4), keepdims=True)
        s = jnp.var(g, axis=(2, 3, 4), keepdims=True)
        return ((g - m) / jnp.sqrt(s + eps)).reshape(v.shape)

    def _ln_c(v, eps=1e-6):
        m = jnp.mean(v, axis=1, keepdims=True)
        s = jnp.var(v, axis=1, keepdims=True)
        return (v - m) / jnp.sqrt(s + eps)

    def _ln_t(v, eps=1e-5):
        m = jnp.mean(v, axis=-1, keepdims=True)
        s = jnp.var(v, axis=-1, keepdims=True)
        return (v - m) / jnp.sqrt(s + eps)

    def _to_tokens(v):
        B_, C_, H_, W_ = v.shape
        return v.reshape(B_, C_, H_ * W_).transpose(0, 2, 1)
    def _from_tokens(t, like):
        B_, C_, H_, W_ = like.shape
        return t.transpose(0, 2, 1).reshape(B_, C_, H_, W_)

    x = _L0_conv_ref(x, L0_conv_b0, L0_conv_w, L0_conv_gamma, L0_conv_beta, L0_conv_b1, L0_conv_alpha, L0_conv_b2)
    x = _L1_conv_ref(x, L1_conv_sw, L1_conv_sb, L1_conv_cw1, L1_conv_cb1, L1_conv_cw2, L1_conv_cb2, L1_conv_w2, L1_conv_b2)
    return x


_drawn_inputs = setup_inputs


def setup_inputs(seed=0):
    import zlib

    import numpy as np

    out = dict(_drawn_inputs(seed))
    spreads = {'L0_conv_b0': (0.0, 0.1),
     'L0_conv_gamma': (1.0, 0.2),
     'L0_conv_beta': (0.0, 0.1),
     'L0_conv_b1': (0.0, 0.1),
     'L0_conv_alpha': (0.25, 0.2),
     'L0_conv_b2': (0.0, 0.1)}
    factors = {}
    for name, (base, spread) in spreads.items():
        noise = np.random.default_rng([zlib.crc32(name.encode()), seed]).standard_normal(out[name].shape)
        drawn = base * np.exp(spread * noise) if base else spread * noise
        out[name] = jnp.asarray(drawn.astype(out[name].dtype))
    for name, factor in factors.items():
        out[name] = (out[name] * factor).astype(out[name].dtype)
    return out
```

```python
import concourse.bass as bass
from concourse import mybir
from contextlib import ExitStack


def build(nc, x, b0, w0, gamma, beta, b1, alpha, b2, sw, sb, cw1, cb1, cw2, cb2, w2, bias2, out):
    fp32, fp32r = mybir.dt.float32, mybir.dt.float32r
    bf16, fp16 = mybir.dt.bfloat16, mybir.dt.float16
    ALU, ACT, AX = mybir.AluOpType, mybir.ActivationFunctionType, mybir.AxisListType
    ds = bass.ds

    B, C, H, W = x.shape
    K = 3
    TAPS = K * K
    MID = cw1.shape[0]
    PAIRS = B // 2
    ROWS = 8
    HR = ROWS // 2
    CHUNKS = H // ROWS
    UNITS = CHUNKS // 2
    TOTAL = PAIRS * CHUNKS
    HP, WP = H + 2, W + 2
    LINE = 128
    FW = w2.shape[3]
    FPAD = FW // 2
    WA = W + FW - 1
    FP = (FW + 1) // 2
    PARTS = 2
    SROW = 2 * TAPS
    UROW = PARTS * SROW
    RING = 6
    ADDS = TAPS - 2
    LEAD = CHUNKS + 2
    USLOTS = 16
    UPAD = 66
    BN_EPS = 1e-5
    STD2 = 2.0 / (K * K)
    HALVES = ((0, C), (C, 2 * C))

    x_v = x.rearrange("(n i) c h w -> n (i c) h w", i=2)
    out_v = out.rearrange("(n i) c h w -> n (i c) h w", i=2)
    sums = nc.dram_tensor("conv_sums", [PAIRS, 2 * C, H, W], fp16, kind="Internal").ap()

    ctx = ExitStack()
    with ctx:
        def sbuf(name, shape, dt=fp32):
            return ctx.enter_context(nc.sbuf_tensor(name, shape, dt))

        def psum(name, shape):
            return ctx.enter_context(nc.psum_tensor(name, shape, fp32))

        def sem(name):
            return ctx.enter_context(nc.semaphore(name))

        x1 = sbuf("x1", [128, 2, HP, WP])
        signs = x1[:, 0, :, :].rearrange("p h w -> p (h w)").bitcast(bf16).rearrange(
            "p (s h w) -> p s h w", s=2, h=HP)
        xin = sbuf("xin", [128, 2, ROWS, W])
        iin = sbuf("iin", [128, 2, ROWS, W], fp16)
        pos = sbuf("pos", [128, ROWS, W])
        y = sbuf("y", [128, 2, ROWS, W])
        prod = sbuf("prod", [128, RING, ROWS, W])
        stats = prod[:, :, :, :].rearrange("p a h w -> p (a h w)").rearrange("p (g s) -> p g s", s=6)
        z = sbuf("z", [128, 2, ROWS, W])
        xa = sbuf("xa", [128, 2, ROWS, WA])
        xb = sbuf("xb", [128, 2, ROWS, WA])
        fin = sbuf("fin", [128, 2, ROWS, W])
        tc = sbuf("tc", [W, 2, ROWS, 2, TAPS])
        tsq = sbuf("tsq", [W, ROWS, 2, TAPS])
        tss = sbuf("tss", [W, 2, ROWS, 2])
        tsd = sbuf("tsd", [W, 2, ROWS, 2])
        trs = sbuf("trs", [W, 2, ROWS, 2])
        u = sbuf("u", [W, USLOTS, ROWS, SROW])
        us = sbuf("us", [W, 2, ROWS, UPAD], fp32r)
        ut = sbuf("ut", [128, 2, ROWS, W], fp32r)
        fin_f = fin[:, :, :, :].rearrange("p s h w -> p (s h w)")
        z_f = z[:, :, :, :].rearrange("p s h w -> p (s h w)")
        CT = C * TAPS
        wraw = fin_f[:, 0:CT].rearrange("p (o k) -> p o k", k=TAPS)
        wabs = fin_f[:, CT:2 * CT]
        ident_f = fin_f[:, 2 * CT:2 * CT + 128]
        avg = fin_f[:, 2 * CT + 128:2 * CT + 256]
        w2raw = z_f[:, 0:C * FW].rearrange("p (o k) -> p o k", k=FW)
        wbin = y[:, 1].rearrange("p r w -> p (r w)")[:, 0:TAPS * 64].bitcast(bf16).rearrange("p (k c) -> p k c", k=TAPS)
        b2wide, ones, swraw = y[:, 0, 0, :], y[0:1, 0, 1, :], y[:, 0, 2, 0:TAPS]
        sel_f = z_f[:, C * FW:C * FW + TAPS * 128].rearrange("p (k c) -> p k c", k=TAPS)
        w2t = sbuf("w2t", [128, 2, FP, C])
        ident = sbuf("ident", [128, 128], fp32r)
        sel = sbuf("sel", [128, TAPS, 128], fp32r)
        swbd = sbuf("swbd", [128, SROW])
        sbrow = sbuf("sbrow", [1, 2, TAPS])
        sbc = sbuf("sbc", [1, 2, TAPS])
        tbias = sbuf("tbias", [W, 2, TAPS])
        cw1t = sbuf("cw1t", [128, MID])
        cb1c = sbuf("cb1c", [MID, 1])
        cw2t = sbuf("cw2t", [MID + 1, 128, TAPS])
        h1 = sbuf("h1", [MID + 1, 2])
        NPAR = 7
        par = sbuf("par", [128, NPAR])
        P_B0, P_GAMMA, P_BETA, P_B1, P_ALPHA, P_B2, P_BIAS2 = (par[:, i:i + 1] for i in range(NPAR))
        col = sbuf("col", [128, 24])
        names = ["wsum", "scale", "mean", "var", "gmean", "gvar", "d", "d2", "v", "sv", "ve", "sd", "r", "e1",
                 "e2", "e3", "e4", "A", "mA", "Bc", "nB", "nalpha", "negm", "cs"]
        cl = {k: col[:, i:i + 1] for i, k in enumerate(names)}
        gs = sbuf("gs", [128, 2, CHUNKS])
        g2 = sbuf("g2", [128, 2])
        cf = sbuf("cf", [128, TAPS])
        cfc = sbuf("cfc", [128, TAPS])
        cfq = sbuf("cfq", [128, TAPS])
        cfn = sbuf("cfn", [128, TAPS])
        cft = sbuf("cft", [128, 4])

        wide = psum("wide", [128, 2, ROWS, LINE])
        acc = psum("acc", [128, ROWS, LINE])
        pt = psum("pt", [128, 512])
        pu = psum("pu", [128, 512])
        pt_v = pt[0:W, 0:ROWS * SROW].rearrange("p (r a k) -> p r a k", r=ROWS, a=2)

        w_loaded, par_loaded, aux_loaded = sem("w_loaded"), sem("par_loaded"), sem("aux_loaded")
        x_loaded = [sem(f"x_loaded{i}") for i in range(2)]
        sums_stored = [sem(f"sums_stored{i}") for i in range(2)]
        in_loaded = [sem(f"in_loaded{i}") for i in range(2)]
        out_stored = [sem(f"out_stored{i}") for i in range(2)]
        pads_zero, chain = sem("pads_zero"), sem("chain")
        const_made, wbin_ready, setup_ready = sem("const_made"), sem("wbin_ready"), sem("setup_ready")
        pool_step, tb_ready, agg_ready, avg_ready = sem("pool_step"), sem("tb_ready"), sem("agg_ready"), sem("avg_ready")
        bn_var, bn_sqrt, bn_ready = sem("bn_var"), sem("bn_sqrt"), sem("bn_ready")
        signed, conv0_done, evacuated, counted = sem("signed"), sem("conv0_done"), sem("evacuated"), sem("counted")
        z0_ready, relus_done, y_ready, x1_ready = sem("z0_ready"), sem("relus_done"), sem("y_ready"), sem("x1_ready")
        t_ready, tc_done, sq_done, ss_done = sem("t_ready"), sem("tc_done"), sem("sq_done"), sem("ss_done")
        sd_done, rs_done, u_done = sem("sd_done"), sem("rs_done"), sem("u_done")
        hi_done, lo_done, turned, ut_ready = sem("hi_done"), sem("lo_done"), sem("turned"), sem("ut_ready")
        wide_ready, products, added = sem("wide_ready"), sem("products"), sem("added")
        leaky_done, spread, conv1_done, fin_ready = sem("leaky_done"), sem("spread"), sem("conv1_done"), sem("fin_ready")
        g_ready, h_ready, h1_ready, cf_raw = sem("g_ready"), sem("h_ready"), sem("h1_ready"), sem("cf_raw")
        cf_var, cf_sqrt, eps_added = sem("cf_var"), sem("cf_sqrt"), sem("eps_added")
        cf_step, cf_end, cf_made, last_two = sem("cf_step"), sem("cf_end"), sem("cf_made"), sem("last_two")

        block = ctx.enter_context(nc.Block())

        def sweep(eng, step):
            step(0, 0, True, False)
            with eng.Fori(1, UNITS) as m:
                step(0, m, False, False)
            with eng.Fori(1, PAIRS - 1) as n:
                with eng.Fori(0, UNITS) as m:
                    step(n, m, False, False)
            with eng.Fori(0, UNITS - 1) as m:
                step(PAIRS - 1, m, False, False)
            step(PAIRS - 1, UNITS - 1, False, True)

        def pipeline(eng, begin, ahead, start, turn, drain):
            begin()
            for s in range(2):
                ahead(0, s, True)
            with eng.Fori(1, LEAD // 2) as unit:
                for s in range(2):
                    ahead(unit * 2, s, False)
            start()

            def turns(n, m, live, more, edge, last):
                for s in range(2):
                    turn(n, m, s, min(3, live + s), more, edge, not (last and s))

            END = UNITS - 1
            turns(0, 0, 0, True, False, False)
            turns(0, 1, 2, True, False, False)
            with eng.Fori(2, END) as m:
                turns(0, m, 3, True, False, False)
            turns(0, END, 3, True, True, False)
            with eng.Fori(1, PAIRS - 2) as n:
                with eng.Fori(0, END) as m:
                    turns(n, m, 3, True, False, False)
                turns(n, END, 3, True, True, False)
            with eng.Fori(0, END) as m:
                turns(PAIRS - 2, m, 3, True, False, False)
            turns(PAIRS - 2, END, 3, False, True, False)
            with eng.Fori(0, END) as m:
                turns(PAIRS - 1, m, 3, False, False, False)
            turns(PAIRS - 1, END, 3, False, False, True)
            drain()

        @block.sync
        def _(sp):
            for lo, hi in HALVES:
                sp.dma_start(wraw[lo:hi, :, :], w0.rearrange("o c a b -> c o (a b)")).then_inc(w_loaded, 16)
                for i, v in enumerate((b0.rearrange("a c h w -> c (a h w)"), gamma.rearrange("(c a) -> c a", a=1),
                                       beta.rearrange("(c a) -> c a", a=1), b1.rearrange("a c h w -> c (a h w)"),
                                       alpha.rearrange("(c a) -> c a", a=1), b2.rearrange("a c h w -> c (a h w)"),
                                       bias2.rearrange("(c a) -> c a", a=1))):
                    sp.dma_start(par[lo:hi, i:i + 1], v).then_inc(par_loaded, 16)

            def load_x(n, m, first, last):
                for s in range(2):
                    if not first:
                        sp.wait_ge(signed, n * CHUNKS + m * 2 + (s - 1))
                    sp.dma_start(xin[:, s], x_v[n, :, ds(m * 2 * ROWS + s * ROWS, ROWS), :]).then_inc(x_loaded[s], 16)

            sweep(sp, load_x)

            sp.wait_ge(signed, TOTAL)
            sp.wait_ge(counted, TOTAL)
            for s in range(2):
                sp.wait_ge(sums_stored[s], 16 * TOTAL // 2)

            def load(t, s, wait):
                if wait is not None:
                    sp.wait_ge(relus_done, wait)
                n, q = (t // CHUNKS, t % CHUNKS)
                sp.dma_start(xin[:, s], x_v[n, :, ds(q * ROWS, ROWS), :]).then_inc(in_loaded[s], 16)
                sp.dma_start(iin[:, s], sums[n, :, ds(q * ROWS, ROWS), :]).then_inc(in_loaded[s], 16)

            def store(t, s, done):
                sp.wait_ge(fin_ready, done * 2)
                n, q = (t // CHUNKS, t % CHUNKS)
                sp.dma_start(out_v[n, :, ds(q * ROWS, ROWS), :], fin[:, s]).then_inc(out_stored[s], 16)

            for s in range(2):
                load(s, s, None)
            FETCH = LEAD + 2
            with sp.Fori(1, FETCH // 2) as unit:
                for s in range(2):
                    load(unit * 2 + s, s, unit * 2 + (s - 1))
            for t in range(4):
                load(t + FETCH, t % 2, t + FETCH - 1)
                if t >= 3:
                    store(t - 3, (t - 3) % 2, t - 2)
            with sp.Fori(2, (TOTAL - FETCH) // 2) as unit:
                for s in range(2):
                    load(unit * 2 + (FETCH + s), s, unit * 2 + (FETCH + s - 1))
                    store(unit * 2 + (s - 3), 1 - s, unit * 2 + (s - 2))
            with sp.Fori((TOTAL - FETCH) // 2, TOTAL // 2 + 1) as unit:
                for s in range(2):
                    store(unit * 2 + (s - 3), 1 - s, unit * 2 + (s - 2))
            store(TOTAL - 1, 1, TOTAL)
            for s in range(2):
                sp.wait_ge(out_stored[s], 16 * TOTAL // 2)

        @block.gpsimd
        def _(pool):
            for i, (t, v) in enumerate(((ident_f[:, :], 0.0), (sel_f[:, :, :], 0.0), (avg[:, :], 0.0),
                                        (g2[:, :], 0.0), (h1[:, :], 1.0), (cw2t[:, :, :], 0.0))):
                nc.gpsimd.memset(t, v).then_inc(pool_step, 1)
            pool.wait_ge(pool_step, 6)
            nc.gpsimd.affine_select(out=ident_f[:, :], in_=ident_f[:, :], compare_op=ALU.not_equal, fill=1.0, base=0,
                                    pattern=[[-1, 128]], channel_multiplier=1).then_inc(pool_step, 1)
            step = 7
            for part in range(PARTS):
                for img in range(2):
                    pool.wait_ge(pool_step, step)
                    v = sel_f[:, :, C * img:C * img + C]
                    nc.gpsimd.affine_select(out=v, in_=v, compare_op=ALU.not_equal, fill=1.0,
                                            base=-(SROW * part + TAPS * img), pattern=[[-1, TAPS], [0, C]],
                                            channel_multiplier=1).then_inc(pool_step, 1)
                    step += 1
            for shift in (0, C, -C):
                pool.wait_ge(pool_step, step)
                nc.gpsimd.affine_select(out=avg[:, :], in_=avg[:, :], compare_op=ALU.not_equal, fill=0.5, base=shift,
                                        pattern=[[-1, 128]], channel_multiplier=1).then_inc(pool_step, 1)
                step += 1
            pool.wait_ge(pool_step, step)
            loads = 0
            for i, (lo, hi) in enumerate(HALVES):
                pool.dma_start(w2raw[lo:hi, :, :], w2.rearrange("o c a k -> c o (a k)"), allow_slow_non_contiguous=True).then_inc(aux_loaded, 16)
                pool.dma_start(wabs[lo:hi, :], w0.rearrange("o c a b -> o (c a b)"), allow_slow_non_contiguous=True).then_inc(aux_loaded, 16)
                pool.dma_start(swraw[lo:hi, :], sw.rearrange("t c -> c t"), allow_slow_non_contiguous=True).then_inc(aux_loaded, 16)
                pool.dma_start(cw1t[lo:hi, :], cw1.rearrange("m c -> c m"), allow_slow_non_contiguous=True).then_inc(aux_loaded, 16)
                pool.dma_start(sbrow[0:1, i, :], sb.rearrange("(a t) -> a t", a=1), allow_slow_non_contiguous=True).then_inc(aux_loaded, 16)
                loads += 5
                pool.dma_start(cw2t[0:MID, lo:hi, :].rearrange("m c k -> m (c k)"), cw2.rearrange("n m -> m n"),
                               allow_slow_non_contiguous=True).then_inc(aux_loaded, 16)
                pool.dma_start(cw2t[MID:MID + 1, lo:hi, :].rearrange("m c k -> m (c k)"),
                               cb2.rearrange("(a n) -> a n", a=1)).then_inc(aux_loaded, 16)
                loads += 2
            pool.dma_start(cb1c[:, :], cb1.rearrange("(c a) -> c a", a=1), allow_slow_non_contiguous=True).then_inc(aux_loaded, 16)
            loads += 1
            pool.wait_ge(aux_loaded, 16 * loads)
            nc.gpsimd.memset(ones[:, :], 1.0).then_inc(const_made, 1)

            def store_sums(n, m, first, last):
                for s in range(2):
                    pool.wait_ge(evacuated, n * CHUNKS + m * 2 + (s + 1))
                    pool.dma_start(sums[n, :, ds(m * 2 * ROWS + s * ROWS, ROWS), :], iin[:, s])\
                        .then_inc(sums_stored[s], 16)

            sweep(pool, store_sums)

            def norm_filter(t, s):
                pool.wait_ge(rs_done, t + (s + 1))
                o = u[:, (t + s) % USLOTS, :, :].rearrange("p r (a k) -> p r a k", a=2)
                nc.gpsimd.tensor_tensor(o, tc[:, s], trs[:, s].unsqueeze(3).broadcast_to([W, ROWS, 2, TAPS]),
                                        ALU.mult).then_inc(u_done, 1)

            def add_taps(n, m, s, live):
                t = n * CHUNKS + m * 2
                if live >= 2:
                    pool.wait_ge(spread, t + (s - 1))
                for k in range(1, ADDS + 1):
                    if k < ADDS:
                        pool.wait_ge(products, t * TAPS + (s * TAPS + k + 1))
                        tap = k
                    else:
                        pool.wait_ge(last_two, t + (s + 1))
                        tap = TAPS - 1
                    if k > 1:
                        pool.wait_ge(added, t * ADDS + (s * ADDS + k - 1))
                    first = prod[:, (TAPS * s) % RING] if k == 1 else z[:, s]
                    nc.gpsimd.tensor_tensor(z[:, s], first, prod[:, (TAPS * s + tap) % RING], ALU.add)\
                        .then_inc(added, 1)

            def turn(n, m, s, live, more, edge, nxt):
                add_taps(n, m, s, live)
                if more:
                    norm_filter(n * CHUNKS + m * 2 + LEAD, s)

            pipeline(pool, lambda: None, lambda t, s, first: norm_filter(t, s), lambda: None, turn, lambda: None)

        @block.scalar
        def _(act):
            act.wait_ge(pads_zero, 1)
            nc.scalar.activation(cl["e4"], cl["e4"], ACT.Sqrt).then_inc(const_made, 1)
            act.wait_ge(const_made, 2)
            act.wait_ge(pads_zero, 4)
            act.wait_ge(par_loaded, 16 * 2 * NPAR)
            nc.scalar.activation(ident[:, :], ident_f[:, :], ACT.Copy).then_inc(setup_ready, 1)
            nc.scalar.activation(sel[:, :, :], sel_f[:, :, :], ACT.Copy).then_inc(setup_ready, 1)

            def evacuate(t, s, reuse):
                act.wait_ge(conv0_done, t + (s + 1))
                if reuse is not None and reuse is not False:
                    act.wait_ge(counted, t + (s - 1))
                    act.wait_ge(sums_stored[s], reuse)
                nc.scalar.activation(iin[:, s], wide[:, s, :, 0:W], ACT.Copy).then_inc(evacuated, 1)

            def sign_step(n, m, first, last):
                for s in range(2):
                    act.wait_ge(x_loaded[s], n * (16 * UNITS) + m * 16 + 16)
                    nc.scalar.activation(signs[:, n % 2, ds(m * 2 * ROWS + (s * ROWS + 1), ROWS), 1:W + 1], xin[:, s],
                                         ACT.Sign, bias=P_B0).then_inc(signed, 1)
                    if not first:
                        if isinstance(n, int) and n == 0 and peeled["one"]:
                            evacuate(n * CHUNKS + m * 2 - 2, s, None)
                        else:
                            evacuate(n * CHUNKS + m * 2 - 2, s, n * (16 * UNITS) + m * 16 - 16)

            peeled = {"one": False}
            sign_step(0, 0, True, False)
            peeled["one"] = True
            sign_step(0, 1, False, False)
            peeled["one"] = False
            with act.Fori(2, UNITS) as m:
                sign_step(0, m, False, False)
            with act.Fori(1, PAIRS) as n:
                with act.Fori(0, UNITS) as m:
                    sign_step(n, m, False, False)
            for s in range(2):
                evacuate(TOTAL - 2, s, 16 * (TOTAL // 2 - 1))

            def begin():
                act.wait_ge(bn_var, 1)
                nc.scalar.activation(cl["sd"], cl["ve"], ACT.Sqrt).then_inc(bn_sqrt, 1)
                act.wait_ge(bn_ready, 1)

            def relus(t, s, first):
                act.wait_ge(z0_ready, t + (s + 1))
                if not first or s:
                    act.wait_ge(y_ready, t + s)
                if not first:
                    act.wait_ge(t_ready, t + (s - 1))
                    act.wait_ge(x1_ready, t + (s - 1))
                nc.scalar.activation(pos[:, :, :], xin[:, s], ACT.Relu, bias=cl["Bc"])
                nc.scalar.activation(y[:, s], xin[:, s], ACT.Relu, bias=cl["nB"], scale=-1.0).then_inc(relus_done, 1)

            def keep_x1(t, s):
                act.wait_ge(y_ready, t + (s + 1))
                pair, q = (t + s) // CHUNKS, (t + s) % CHUNKS
                nc.scalar.activation(x1[:, pair % 2, ds(q * ROWS + 1, ROWS), 1:W + 1], y[:, s], ACT.Identity, bias=P_B2,
                                     accum_out=gs[:, pair % 2, ds(q, 1)]).then_inc(x1_ready, 1)

            def square(t, s):
                act.wait_ge(tc_done, t + (s + 1))
                nc.scalar.activation(tsq[:, :, :, :], tc[:, s], ACT.Square).then_inc(sq_done, 1)

            def root(t, s):
                act.wait_ge(ss_done, t + (s + 1))
                nc.scalar.activation(tsd[:, s], tss[:, s], ACT.Sqrt, scale=1.0 / (TAPS - 1)).then_inc(sd_done, 1)

            def ahead(t, s, first):
                relus(t, s, first)
                keep_x1(t, s)
                square(t, s)
                root(t, s)

            def high_part(t, o, s, reuse):
                act.wait_ge(u_done, t + (o + 1))
                if reuse:
                    act.wait_ge(turned, t * 2 + 2 * (o - 1))
                nc.scalar.activation(us[:, s, :, 0:SROW], u[:, (t + o) % USLOTS, :, :], ACT.Copy).then_inc(hi_done, 1)

            def take_turned(t, o, s, h):
                act.wait_ge(turned, t * 2 + (2 * o + h + 1))
                nc.scalar.activation(ut[0:UROW, s, HR * h:HR * h + HR, :],
                                     pu[0:UROW, 0:HR * W].rearrange("p (r w) -> p r w", r=HR), ACT.Copy)\
                    .then_inc(ut_ready, 1)

            def spread_rows(t, o, s, half, reuse):
                if half == 0:
                    act.wait_ge(leaky_done, t + (o + 1))
                    if reuse:
                        act.wait_ge(conv1_done, t * 2 + 2 * (o - 1))
                a, b = (0, 64), (64, 128)
                dst, d, at, src = ((xa, a, FPAD, a), (xa, b, FPAD - 1, a), (xb, b, FPAD, b), (xb, a, FPAD - 1, b))[half]
                i = nc.scalar.activation(dst[d[0]:d[1], s, :, at:at + W], z[src[0]:src[1], s], ACT.Copy)
                if half == 3:
                    i.then_inc(spread, 1)

            def finish(t, o, s, h, reuse):
                act.wait_ge(conv1_done, t * 2 + (2 * o + h + 1))
                if h == 0 and reuse:
                    act.wait_ge(out_stored[s], t * 8 + (16 * ((o - 2 - s) // 2) + 16))
                nc.scalar.activation(fin[:, s, HR * h:HR * h + HR, :], acc[:, HR * h:HR * h + HR, 0:W], ACT.Identity,
                                     bias=P_BIAS2).then_inc(fin_ready, 1)

            def hidden(pair):
                act.wait_ge(h_ready, pair + 1)
                nc.scalar.activation(h1[0:MID, :], pt[0:MID, 0:2], ACT.Relu, bias=cb1c[:, :], scale=1.0 / (H * W))\
                    .then_inc(h1_ready, 1)

            def cf_root(pair):
                act.wait_ge(cf_var, pair + 1)
                nc.scalar.activation(cft[:, 2:3], cft[:, 1:2], ACT.Sqrt, scale=1.0 / (TAPS - 1)).then_inc(cf_sqrt, 1)

            def turn(n, m, s, live, more, edge, nxt):
                t = n * CHUNKS + m * 2
                if nxt:
                    high_part(t, s + 1, 1 - s, live >= 1)
                if live >= 3:
                    finish(t, s - 3, 1 - s, 1, True)
                if more:
                    relus(t + LEAD, s, False)
                    keep_x1(t + LEAD, s)
                if nxt:
                    take_turned(t, s + 1, 1 - s, 0)
                    take_turned(t, s + 1, 1 - s, 1)
                if live >= 2:
                    finish(t, s - 2, s, 0, not (isinstance(n, int) and n == 0 and isinstance(m, int) and m < 2))
                if edge and s == 1:
                    cf_root(n + 1)
                for half in range(4):
                    if live >= 1:
                        spread_rows(t, s - 1, 1 - s, half, live >= 3)
                if more:
                    square(t + LEAD, s)
                    root(t + LEAD, s)
                if edge and s == 0:
                    hidden(n + 1)

            def start():
                hidden(0)
                cf_root(0)
                high_part(0, 0, 0, False)
                take_turned(0, 0, 0, 0)
                take_turned(0, 0, 0, 1)

            def drain():
                finish(TOTAL, -3, 1, 1, True)
                for half in range(4):
                    spread_rows(TOTAL, -1, 1, half, True)
                for h in range(2):
                    finish(TOTAL, -2, 0, h, True)
                for h in range(2):
                    finish(TOTAL, -1, 1, h, True)

            pipeline(act, begin, ahead, start, turn, drain)

        @block.vector
        def _(dve):
            links = [0]

            def link(i):
                links[0] += 1
                i.then_inc(chain, 1)
                dve.wait_ge(chain, links[0])

            nc.vector.memset(col[:, :], 0.0).then_inc(pads_zero, 1)
            nc.vector.memset(ut[:, :, :, :].bitcast(fp32), 0.0)
            nc.vector.memset(us[:, :, :, :].bitcast(fp32), 0.0).then_inc(pads_zero, 1)
            nc.vector.memset(x1[:, 0, :, :], 0.0).then_inc(pads_zero, 1)
            nc.vector.memset(xa[:, :, :, :], 0.0)
            nc.vector.memset(xb[:, :, :, :], 0.0)
            link(nc.vector.memset(wbin[:, :, :], 0.0))
            link(nc.vector.memset(swbd[:, :], 0.0))
            link(nc.vector.memset(w2t[:, :, :, :], 0.0))
            nc.vector.memset(b2wide[:, :], 1.0).then_inc(pads_zero, 1)
            dve.wait_ge(w_loaded, 32)
            link(nc.vector.tensor_scalar(wraw[:, :, :], wraw[:, :, :], 0.0, 2.0, ALU.is_gt, ALU.mult))
            for lo, hi in HALVES:
                last = nc.vector.tensor_scalar(wbin[lo:hi, :, lo:hi], wraw[lo:hi, :, :].rearrange("c o k -> c k o"),
                                               -1.0, None, ALU.add)
                last.then_inc(wbin_ready, 1)
            dve.wait_ge(const_made, 2)
            dve.wait_ge(par_loaded, 16 * 2 * NPAR)
            dve.wait_ge(pads_zero, 4)
            link(nc.vector.scalar_tensor_tensor(wabs[:, :], wabs[:, :], -1.0, wabs[:, :], ALU.mult, ALU.max))
            link(nc.vector.tensor_reduce(cl["wsum"], wabs[:, :], AX.X, ALU.add))
            link(nc.vector.tensor_scalar(cl["scale"], cl["wsum"], 1.0 / (C * TAPS), None, ALU.mult))
            link(nc.vector.tensor_reduce(cl["cs"], swraw[:, :], AX.X, ALU.add))
            link(nc.vector.tensor_scalar(cl["negm"], cl["cs"], -1.0 / TAPS, None, ALU.mult))
            for i, (lo, hi) in enumerate(HALVES):
                link(nc.vector.tensor_scalar(swbd[lo:hi, TAPS * i:TAPS * i + TAPS], swraw[lo:hi, :],
                                             cl["negm"][lo:hi, :], None, ALU.add))
            link(nc.vector.tensor_reduce(sbc[0:1, 0, 0:1], sbrow[0:1, 0, :], AX.X, ALU.add))
            link(nc.vector.tensor_scalar(sbc[0:1, 0, 1:2], sbc[0:1, 0, 0:1], -1.0 / TAPS, None, ALU.mult))
            link(nc.vector.tensor_scalar(sbrow[0:1, :, :], sbrow[0:1, :, :], sbc[0:1, 0, 1:2], None, ALU.add))
            link(nc.vector.tensor_scalar(b2wide[:, :], b2wide[:, :], P_B2, None, ALU.mult))
            link(nc.vector.tensor_scalar(cl["nalpha"], P_ALPHA, -1.0, None, ALU.mult))
            for lo, hi in HALVES:
                img = lo // C
                olo, ohi = C - lo, 2 * C - lo
                link(nc.vector.tensor_copy(w2t[lo:hi, img, :, :], w2raw[lo:hi, :, 0:FW:2].rearrange("c o k -> c k o")))
                link(nc.vector.tensor_copy(w2t[olo:ohi, img, 0:FP - 1, :],
                                           w2raw[olo:ohi, :, 1:FW:2].rearrange("c o k -> c k o")))
            nc.vector.memset(cft[:, :], 0.0).then_inc(setup_ready, 1)
            dve.wait_ge(tb_ready, 1)
            nc.vector.tensor_copy(tbias[:, :, :], pt[0:W, 0:SROW].rearrange("p (a k) -> p a k", a=2))\
                .then_inc(setup_ready, 1)

            def count(n, m, first, last):
                for s in range(2):
                    dve.wait_ge(evacuated, n * CHUNKS + m * 2 + (s + 1))
                    for h in range(2):
                        i = nc.vector.bn_stats(stats[:, ds(n * (2 * CHUNKS) + m * 4 + (2 * s + h), 1), :].rearrange("p a s -> p (a s)"),
                                               iin[:, s, HR * h:HR * h + HR, :])
                    i.then_inc(counted, 1)

            sweep(dve, count)

            def begin():
                dve.wait_ge(counted, TOTAL)
                link(nc.vector.bn_aggr(col[:, 2:4], stats[:, 0:2 * TOTAL, :]))
                nc.vector.memset(x1[:, :, 0:1, :], 0.0)
                nc.vector.memset(x1[:, :, HP - 1:HP, :], 0.0)
                nc.vector.memset(x1[:, :, 1:HP - 1, 0:1], 0.0)
                link(nc.vector.memset(x1[:, :, 1:HP - 1, WP - 1:WP], 0.0))
                nc.vector.tensor_scalar(cl["e4"], cl["mean"], 1.0, None, ALU.mult).then_inc(agg_ready, 1)
                dve.wait_ge(avg_ready, 1)
                link(nc.vector.tensor_copy(col[:, 4:6], pt[:, 0:2]))
                link(nc.vector.tensor_tensor(cl["d"], cl["mean"], cl["gmean"], ALU.subtract))
                link(nc.vector.tensor_tensor(cl["d2"], cl["d"], cl["d"], ALU.mult))
                link(nc.vector.tensor_tensor(cl["v"], cl["gvar"], cl["d2"], ALU.add))
                link(nc.vector.tensor_tensor(cl["sv"], cl["v"], cl["scale"], ALU.mult))
                link(nc.vector.tensor_scalar(cl["ve"], cl["sv"], cl["scale"], BN_EPS, ALU.mult, ALU.add))
                nc.vector.tensor_copy(cl["e1"], cl["ve"]).then_inc(bn_var, 1)
                dve.wait_ge(bn_sqrt, 1)
                link(nc.vector.reciprocal(cl["r"], cl["sd"]))
                link(nc.vector.tensor_tensor(cl["e2"], cl["r"], cl["r"], ALU.mult))
                link(nc.vector.tensor_tensor(cl["e3"], cl["e2"], cl["ve"], ALU.mult))
                link(nc.vector.tensor_scalar(cl["e2"], cl["e3"], -0.5, 1.5, ALU.mult, ALU.add))
                link(nc.vector.tensor_tensor(cl["e3"], cl["e2"], cl["r"], ALU.mult))
                link(nc.vector.tensor_tensor(cl["e2"], cl["e3"], cl["scale"], ALU.mult))
                link(nc.vector.tensor_tensor(cl["A"], cl["e2"], P_GAMMA, ALU.mult))
                link(nc.vector.tensor_tensor(cl["mA"], cl["gmean"], cl["A"], ALU.mult))
                link(nc.vector.tensor_tensor(cl["e3"], P_BETA, cl["mA"], ALU.subtract))
                link(nc.vector.tensor_tensor(cl["Bc"], cl["e3"], P_B1, ALU.add))
                link(nc.vector.tensor_scalar(cl["nB"], cl["Bc"], -1.0, None, ALU.mult))
                nc.vector.tensor_copy(cl["e2"], cl["nB"]).then_inc(bn_ready, 1)

            def add_residual(t, s):
                dve.wait_ge(in_loaded[s], t * 16 + 32)
                nc.vector.scalar_tensor_tensor(xin[:, s], iin[:, s], cl["A"], xin[:, s], ALU.mult, ALU.add)\
                    .then_inc(z0_ready, 1)

            def prelu(t, s):
                dve.wait_ge(relus_done, t + (s + 1))
                nc.vector.scalar_tensor_tensor(y[:, s], y[:, s], cl["nalpha"], pos[:, :, :], ALU.mult, ALU.add)\
                    .then_inc(y_ready, 1)

            def centre(t, s, first):
                dve.wait_ge(t_ready, t + (s + 1))
                if not first:
                    dve.wait_ge(u_done, t + (s - 1))
                nc.vector.tensor_tensor(tc[:, s], pt_v, tbias[:, :, :].unsqueeze(1).broadcast_to([W, ROWS, 2, TAPS]),
                                        ALU.add).then_inc(tc_done, 1)

            def sum_squares(t, s):
                dve.wait_ge(sq_done, t + (s + 1))
                nc.vector.tensor_reduce(tss[:, s], tsq[:, :, :, :], AX.X, ALU.add).then_inc(ss_done, 1)

            def inverse(t, s):
                dve.wait_ge(sd_done, t + (s + 1))
                nc.vector.tensor_scalar(tsd[:, s], tsd[:, s], 1e-10, None, ALU.add).then_inc(eps_added, 1)
                dve.wait_ge(eps_added, t + (s + 1))
                nc.vector.reciprocal(trs[:, s], tsd[:, s]).then_inc(rs_done, 1)

            def ahead(t, s, first):
                add_residual(t, s)
                prelu(t, s)
                centre(t, s, first)
                sum_squares(t, s)
                inverse(t, s)

            def low_part(t, o, s):
                dve.wait_ge(hi_done, t + (o + 1))
                nc.vector.tensor_tensor(us[:, s, :, SROW:UROW], u[:, (t + o) % USLOTS, :, :],
                                        us[:, s, :, 0:SROW].bitcast(fp32), ALU.subtract).then_inc(lo_done, 1)

            USED_BY = {0: 3, 1: 4, 2: 5, 3: 6, 5: ADDS, 6: 1, 7: 1, 8: 2}

            def product(n, m, s, k, live):
                t = n * CHUNKS + m * 2
                if k == 0:
                    dve.wait_ge(cf_made, n + 1)
                if k == 4 and live:
                    dve.wait_ge(last_two, t + s)
                elif k != 4 and (live or k >= RING):
                    dve.wait_ge(added, t * ADDS + (ADDS * (s if k >= RING else s - 1) + USED_BY[k]))
                dve.wait_ge(wide_ready, t * TAPS + (s * TAPS + k + 1))
                nc.vector.scalar_tensor_tensor(
                    prod[:, (TAPS * s + k) % RING],
                    x1[:, n % 2, ds(m * 2 * ROWS + (s * ROWS + k // K), ROWS), k % K:k % K + W],
                    cfn[:, k:k + 1], wide[:, (TAPS * s + k) % 2, :, 0:W], ALU.mult, ALU.mult).then_inc(products, 1)

            def add_last_two(n, m, s):
                t = n * CHUNKS + m * 2
                a, b = (TAPS * s + TAPS - 2) % RING, (TAPS * s + TAPS - 1) % RING
                dve.wait_ge(products, t * TAPS + (s + 1) * TAPS)
                nc.vector.tensor_tensor(prod[:, b], prod[:, a], prod[:, b], ALU.add).then_inc(last_two, 1)

            def leaky(t, o, s):
                dve.wait_ge(added, t * ADDS + ADDS * (o + 1))
                nc.vector.scalar_tensor_tensor(z[:, s], z[:, s], 0.1, z[:, s], ALU.mult, ALU.max)\
                    .then_inc(leaky_done, 1)

            def sum_images(pair):
                dve.wait_ge(x1_ready, pair * CHUNKS + CHUNKS)
                nc.vector.tensor_reduce(cft[:, 0:1], gs[:, pair % 2, :], AX.X, ALU.add).then_inc(cf_step, 1)

            def place_sums(pair):
                dve.wait_ge(cf_step, pair * 6 + 1)
                for i, (lo, hi) in enumerate(HALVES):
                    nc.vector.tensor_copy(g2[lo:hi, i:i + 1], cft[lo:hi, 0:1]).then_inc(g_ready, 1)

            def cf_centre(pair):
                dve.wait_ge(cf_raw, pair + 1)
                cfp = pt[:, 64:64 + 2 * TAPS].rearrange("p (k i) -> p k i", i=2)
                for i, (lo, hi) in enumerate(HALVES):
                    nc.vector.tensor_copy(cf[lo:hi, :], cfp[lo:hi, :, i]).then_inc(cf_step, 1)
                dve.wait_ge(cf_step, pair * 6 + 3)
                nc.vector.tensor_reduce(cft[:, 0:1], cf[:, :], AX.X, ALU.add).then_inc(cf_step, 1)
                dve.wait_ge(cf_step, pair * 6 + 4)
                nc.vector.tensor_scalar(cft[:, 3:4], cft[:, 0:1], -1.0 / TAPS, None, ALU.mult).then_inc(cf_step, 1)
                dve.wait_ge(cf_step, pair * 6 + 5)
                nc.vector.tensor_scalar(cfc[:, :], cf[:, :], cft[:, 3:4], None, ALU.add).then_inc(cf_step, 1)

            def cf_squares(pair):
                dve.wait_ge(cf_step, pair * 6 + 6)
                nc.vector.tensor_tensor(cfq[:, :], cfc[:, :], cfc[:, :], ALU.mult).then_inc(cf_end, 1)
                dve.wait_ge(cf_end, pair * 3 + 1)
                nc.vector.tensor_reduce(cft[:, 1:2], cfq[:, :], AX.X, ALU.add).then_inc(cf_var, 1)

            def cf_scale(pair):
                dve.wait_ge(cf_sqrt, pair + 1)
                nc.vector.tensor_scalar(cft[:, 0:1], cft[:, 2:3], 1e-10, None, ALU.add).then_inc(cf_end, 1)
                dve.wait_ge(cf_end, pair * 3 + 2)
                nc.vector.reciprocal(cft[:, 3:4], cft[:, 0:1]).then_inc(cf_end, 1)

            def cf_finish(pair):
                dve.wait_ge(cf_end, pair * 3 + 3)
                nc.vector.tensor_scalar(cfn[:, :], cfc[:, :], cft[:, 3:4], STD2, ALU.mult, ALU.mult)\
                    .then_inc(cf_made, 1)

            def start():
                for step in (sum_images, place_sums, cf_centre, cf_squares, cf_scale, cf_finish):
                    step(0)
                low_part(0, 0, 0)

            def turn(n, m, s, live, more, edge, nxt):
                t = n * CHUNKS + m * 2
                if more:
                    add_residual(t + LEAD, s)
                product(n, m, s, 0, live)
                if edge and s == 0:
                    sum_images(n + 1)
                product(n, m, s, 1, live)
                if edge and s == 0:
                    place_sums(n + 1)
                if nxt:
                    low_part(t, s + 1, 1 - s)
                if more:
                    prelu(t + LEAD, s)
                product(n, m, s, 2, live)
                if edge and s == 1:
                    cf_centre(n + 1)
                product(n, m, s, 3, live)
                if edge and s == 1:
                    cf_squares(n + 1)
                product(n, m, s, 4, live)
                if live >= 1:
                    leaky(t, s - 1, 1 - s)
                product(n, m, s, 5, live)
                product(n, m, s, 6, live)
                if more:
                    centre(t + LEAD, s, False)
                product(n, m, s, 7, live)
                if more:
                    sum_squares(t + LEAD, s)
                if edge and s == 1:
                    cf_scale(n + 1)
                product(n, m, s, 8, live)
                if more:
                    inverse(t + LEAD, s)
                add_last_two(n, m, s)
                if edge and s == 1:
                    cf_finish(n + 1)

            def drain():
                leaky(TOTAL, -1, 1)

            pipeline(dve, begin, ahead, start, turn, drain)

        @block.tensor
        def _(pe):
            pe.wait_ge(setup_ready, 3)
            nc.tensor.matmul(pt[0:W, 0:SROW], b2wide[:, :], swbd[:, :], start=True, stop=False)
            nc.tensor.matmul(pt[0:W, 0:SROW], ones[:, :], sbrow[0:1, :, :].rearrange("p a k -> p (a k)"),
                             start=False, stop=True).then_inc(tb_ready, 1)

            pe.wait_ge(wbin_ready, 2)

            def conv0(n, m, first, last):
                for s in range(2):
                    t = n * CHUNKS + m * 2
                    pe.wait_ge(signed, TOTAL if last and s else t + (s + 2))
                    if not first:
                        pe.wait_ge(evacuated, t + (s - 1))
                    for h in range(2):
                        for k in range(TAPS):
                            i = nc.tensor.matmul(
                                wide[:, s, HR * h:HR * h + HR, 0:W], wbin[:, k, :],
                                signs[:, n % 2, ds(m * 2 * ROWS + (s * ROWS + HR * h + k // K), HR), k % K:k % K + W],
                                start=k == 0, stop=k == TAPS - 1)
                    i.then_inc(conv0_done, 1)

            sweep(pe, conv0)

            def begin():
                pe.wait_ge(setup_ready, 4)
                pe.wait_ge(agg_ready, 1)
                nc.tensor.matmul(pt[:, 0:2], avg[:, :], col[:, 2:4], start=True, stop=True).then_inc(avg_ready, 1)
                pe.wait_ge(bn_ready, 1)
                pe.wait_ge(evacuated, TOTAL)

            def spatial(t, s, first):
                pe.wait_ge(y_ready, t + (s + 1))
                if not first or s:
                    pe.wait_ge(tc_done, t + s)
                spatial_rows(s, 0, ROWS)

            def spatial_rows(s, a, b):
                for r in range(a, b):
                    i = nc.tensor.matmul(pt[0:W, SROW * r:SROW * r + SROW], y[:, s, r, :], swbd[:, :],
                                         start=True, stop=True)
                if b == ROWS:
                    i.then_inc(t_ready, 1)

            def turn_back(t, o, s, h, first):
                if h == 0:
                    pe.wait_ge(lo_done, t + (o + 1))
                if not (first and h == 0):
                    pe.wait_ge(ut_ready, t * 2 + (2 * o + h))
                for r in range(HR):
                    i = nc.tensor.matmul(pu[0:UPAD, W * r:W * r + W], us[:, s, HR * h + r, :], ident[0:W, 0:W],
                                         start=True, stop=True)
                i.then_inc(turned, 1)

            def spread_tap(n, m, s, k, live):
                p = (n * CHUNKS + m * 2) * TAPS
                if k == 0:
                    pe.wait_ge(ut_ready, (n * CHUNKS + m * 2) * 2 + (2 * s + 2))
                if live or k >= 2:
                    pe.wait_ge(products, p + (s * TAPS + k - 1))
                for h in range(2):
                    i = nc.tensor.matmul(wide[:, (TAPS * s + k) % 2, HR * h:HR * h + HR, 0:W], sel[:, k, :],
                                         ut[:, s, HR * h:HR * h + HR, :], start=True, stop=True)
                i.then_inc(wide_ready, 1)

            def conv1(t, o, s, a, b, reuse):
                c = t + o
                for j in range(a, b):
                    h, i = j // BANK1, j % BANK1
                    if j == 0:
                        pe.wait_ge(spread, t + (o + 1))
                    if i == 0:
                        if reuse:
                            pe.wait_ge(fin_ready, t * 2 + (2 * o + h - 1))
                        nc.tensor.matmul(
                            acc[:, HR * h:HR * h + HR, 0:W], ident[:, :].bitcast(fp32),
                            x1[:, (c // CHUNKS) % 2, ds((c % CHUNKS) * ROWS + (HR * h + 1), HR), 1:W + 1],
                            start=True, stop=False)
                        continue
                    p, img = (i - 1) // 2, (i - 1) % 2
                    src = (xa, xb)[img]
                    mm = nc.tensor.matmul(acc[C * img:C * img + C, HR * h:HR * h + HR, 0:W], w2t[:, img, p, :],
                                          src[:, s, HR * h:HR * h + HR, 2 * p:2 * p + W],
                                          start=False, stop=p == FP - 1)
                    if i == BANK1 - 1:
                        mm.then_inc(conv1_done, 1)

            BANK1 = 2 * FP + 1
            cuts = [0, 3, 7, 10, 12, 14, 16, 18, 20, 22]

            def hidden(pair):
                pe.wait_ge(g_ready, pair * 2 + 2)
                nc.tensor.matmul(pt[0:MID, 0:2], cw1t[:, :], g2[:, :], start=True, stop=True).then_inc(h_ready, 1)

            def channel(pair):
                pe.wait_ge(h1_ready, pair + 1)
                for k in range(TAPS):
                    i = nc.tensor.matmul(pt[:, 64 + 2 * k:66 + 2 * k], cw2t[:, :, k], h1[:, :], start=True, stop=True)
                i.then_inc(cf_raw, 1)

            def turn(n, m, s, live, more, edge, nxt):
                t = n * CHUNKS + m * 2
                for k in range(TAPS):
                    spread_tap(n, m, s, k, live)
                    if k == 1 and edge and s == 1:
                        channel(n + 1)
                    if k == 3 and more:
                        if edge and s == 1:
                            pe.wait_ge(cf_var, n + 2)
                        pe.wait_ge(y_ready, t + (LEAD + s + 1))
                        pe.wait_ge(tc_done, t + (LEAD + s))
                    if 3 <= k < 7 and more:
                        spatial_rows(s, 2 * k - 6, 2 * k - 4)
                    if k == 8 and edge and s == 0:
                        if more:
                            pe.wait_ge(tc_done, t + (LEAD + 1))
                        hidden(n + 1)
                    if live >= 2:
                        conv1(t, s - 2, s, cuts[k], cuts[k + 1], live >= 3)
                    if k == 2 and nxt:
                        turn_back(t, s + 1, 1 - s, 0, False)
                    if k == 4 and nxt:
                        turn_back(t, s + 1, 1 - s, 1, False)

            def start():
                pe.wait_ge(tc_done, LEAD)
                hidden(0)
                channel(0)
                turn_back(0, 0, 0, 0, True)
                turn_back(0, 0, 0, 1, True)
                pe.wait_ge(cf_var, 1)

            def drain():
                conv1(TOTAL, -2, 0, 0, 2 * BANK1, True)
                conv1(TOTAL, -1, 1, 0, 2 * BANK1, True)

            pipeline(pe, begin, spatial, start, turn, drain)


_INS = ["x", "L0_conv_b0", "L0_conv_w", "L0_conv_gamma", "L0_conv_beta", "L0_conv_b1", "L0_conv_alpha", "L0_conv_b2",
        "L1_conv_sw", "L1_conv_sb", "L1_conv_cw1", "L1_conv_cb1", "L1_conv_cw2", "L1_conv_cb2", "L1_conv_w2",
        "L1_conv_b2"]


def kernel(**inputs):
    import numpy as _np
    import concourse.bacc as _bacc
    from concourse import mybir as _mybir
    from concourse.bass_utils import run_bass_kernel_spmd as _run

    nc = _bacc.Bacc("TRN2", target_bir_lowering=False, num_devices=1)
    arrays, args = {}, []
    for name in _INS:
        a = _np.ascontiguousarray(inputs[name])
        arrays[f"in_{name}"] = a
        args.append(nc.dram_tensor(f"in_{name}", a.shape, _mybir.dt.from_np(a.dtype), kind="ExternalInput").ap())
    out = nc.dram_tensor("out", inputs["x"].shape, _mybir.dt.float32, kind="ExternalOutput").ap()
    build(nc, *args, out)
    r = _run(nc, [arrays], core_ids=[0])
    return r.results[0]["out"]
```

```python
import concourse.bass as bass
from concourse import mybir
from contextlib import ExitStack


def build(nc, x, b0, w0, gamma, beta, b1, alpha, b2, sw, sb, cw1, cb1, cw2, cb2, w2, bias2, out):
    fp32, fp32r = mybir.dt.float32, mybir.dt.float32r
    bf16, fp16 = mybir.dt.bfloat16, mybir.dt.float16
    ALU, ACT, AX = mybir.AluOpType, mybir.ActivationFunctionType, mybir.AxisListType
    ds = bass.ds

    B, C, H, W = x.shape
    K = 3
    TAPS = K * K
    MID = cw1.shape[0]
    PAIRS = B // 2
    ROWS = 8
    HR = ROWS // 2
    CHUNKS = H // ROWS
    UNITS = CHUNKS // 2
    TOTAL = PAIRS * CHUNKS
    HP, WP = H + 2, W + 2
    LINE = 128
    FW = w2.shape[3]
    FPAD = FW // 2
    WA = W + FW - 1
    FP = (FW + 1) // 2
    PARTS = 2
    SROW = 2 * TAPS
    UROW = PARTS * SROW
    RING = 6
    ADDS = TAPS - 2
    LEAD = CHUNKS + 2
    USLOTS = 16
    UPAD = 66
    BN_EPS = 1e-5
    STD2 = 2.0 / (K * K)
    HALVES = ((0, C), (C, 2 * C))

    x_v = x.rearrange("(n i) c h w -> n (i c) h w", i=2)
    out_v = out.rearrange("(n i) c h w -> n (i c) h w", i=2)
    sums = nc.dram_tensor("conv_sums", [PAIRS, 2 * C, H, W], fp16, kind="Internal").ap()

    ctx = ExitStack()
    with ctx:
        def sbuf(name, shape, dt=fp32):
            return ctx.enter_context(nc.sbuf_tensor(name, shape, dt))

        def psum(name, shape):
            return ctx.enter_context(nc.psum_tensor(name, shape, fp32))

        def sem(name):
            return ctx.enter_context(nc.semaphore(name))

        x1 = sbuf("x1", [128, 2, HP, WP])
        signs = [x1[:, i, :, :].rearrange("p h w -> p (h w)")[:, 0:HP * WP // 2].bitcast(bf16).rearrange(
            "p (h w) -> p h w", h=HP) for i in range(2)]
        xin = sbuf("xin", [128, 2, ROWS, W])
        iin = sbuf("iin", [128, 2, ROWS, W], fp16)
        y = sbuf("y", [128, 2, ROWS, W])
        prod = sbuf("prod", [128, RING, ROWS, W])
        stats = prod[:, :, :, :].rearrange("p a h w -> p (a h w)").rearrange("p (g s) -> p g s", s=6)
        z = sbuf("z", [128, 2, ROWS, W])
        part = sbuf("part", [128, ROWS, W])
        xa = sbuf("xa", [128, 2, ROWS, WA])
        xb = sbuf("xb", [128, 2, ROWS, WA])
        fin = sbuf("fin", [128, 2, ROWS, W])
        tc = sbuf("tc", [W, 2, ROWS, 2, TAPS])
        tsq = sbuf("tsq", [W, ROWS, 2, TAPS])
        tss = sbuf("tss", [W, 2, ROWS, 2])
        tsd = sbuf("tsd", [W, 2, ROWS, 2])
        trs = sbuf("trs", [W, 2, ROWS, 2])
        u = sbuf("u", [W, USLOTS, ROWS, SROW])
        us = sbuf("us", [W, 2, ROWS, UPAD], fp32r)
        ut = sbuf("ut", [128, 2, ROWS, W], fp32r)
        fin_f = fin[:, :, :, :].rearrange("p s h w -> p (s h w)")
        z_f = z[:, :, :, :].rearrange("p s h w -> p (s h w)")
        CT = C * TAPS
        wraw = fin_f[:, 0:CT].rearrange("p (o k) -> p o k", k=TAPS)
        wabs = fin_f[:, CT:2 * CT]
        ident_f = fin_f[:, 2 * CT:2 * CT + 128]
        avg = fin_f[:, 2 * CT + 128:2 * CT + 256]
        w2raw = z_f[:, 0:C * FW].rearrange("p (o k) -> p o k", k=FW)
        wbin = y[:, 1].rearrange("p r w -> p (r w)")[:, 0:2 * K * C].bitcast(bf16).rearrange(
            "p (i k c) -> p i k c", i=2, k=2 * K)
        shift_wide, ones, swraw = y[:, 0, 0, :], y[0:1, 0, 1, :], y[:, 0, 2, 0:TAPS]
        sel_f = z_f[:, C * FW:C * FW + TAPS * 128].rearrange("p (k c) -> p k c", k=TAPS)
        w2t = sbuf("w2t", [128, 2, FP, C])
        ident = sbuf("ident", [128, 128], fp32r)
        sel = sbuf("sel", [128, TAPS, 128], fp32r)
        swbd = sbuf("swbd", [128, SROW])
        sbrow = sbuf("sbrow", [1, 2, TAPS])
        sbc = sbuf("sbc", [1, 2, TAPS])
        tbias = sbuf("tbias", [W, 2, TAPS])
        cw1t = sbuf("cw1t", [128, MID])
        cb1c = sbuf("cb1c", [MID, 1])
        cw2t = sbuf("cw2t", [MID + 1, 128, TAPS])
        h1 = sbuf("h1", [MID + 1, 2])
        NPAR = 7
        par = sbuf("par", [128, NPAR])
        P_B0, P_GAMMA, P_BETA, P_B1, P_ALPHA, P_B2, P_BIAS2 = (par[:, i:i + 1] for i in range(NPAR))
        col = sbuf("col", [128, 26])
        names = ["wsum", "scale", "mean", "var", "gmean", "gvar", "d", "d2", "v", "sv", "ve", "sd", "r", "e1",
                 "e2", "e3", "e4", "A", "mA", "Bc", "nB", "rise", "negm", "cs", "shift", "tiny"]
        cl = {k: col[:, i:i + 1] for i, k in enumerate(names)}
        gs = sbuf("gs", [128, 2, CHUNKS])
        g2 = sbuf("g2", [128, 2])
        cf = sbuf("cf", [128, TAPS])
        cfc = sbuf("cfc", [128, TAPS])
        cfq = sbuf("cfq", [128, TAPS])
        cfn = sbuf("cfn", [128, TAPS])
        cft = sbuf("cft", [128, 4])

        wide = psum("wide", [128, 2, ROWS, LINE])
        acc = psum("acc", [128, ROWS, LINE])
        pt = psum("pt", [128, 512])
        pu = psum("pu", [128, 512])
        pt_v = pt[0:W, 0:ROWS * SROW].rearrange("p (r a k) -> p r a k", r=ROWS, a=2)

        w_loaded, b0_loaded, par_loaded, aux_loaded = sem("w_loaded"), sem("b0_loaded"), sem("par_loaded"), sem("aux_loaded")
        x_loaded = [[sem(f"x_loaded{i}_{img}") for img in range(2)] for i in range(2)]
        sums_stored = [sem(f"sums_stored{i}") for i in range(2)]
        in_loaded = [sem(f"in_loaded{i}") for i in range(2)]
        out_stored = [sem(f"out_stored{i}") for i in range(2)]
        pads_zero, chain = sem("pads_zero"), sem("chain")
        const_made, wbin_ready, setup_ready = sem("const_made"), sem("wbin_ready"), sem("setup_ready")
        pool_step, tb_ready, agg_ready, avg_ready = sem("pool_step"), sem("tb_ready"), sem("agg_ready"), sem("avg_ready")
        bn_var, bn_sqrt, bn_ready = sem("bn_var"), sem("bn_sqrt"), sem("bn_ready")
        signed, shifted, conv0_done = sem("signed"), sem("shifted"), sem("conv0_done")
        upper_out, lower_out, counted = sem("upper_out"), sem("lower_out"), sem("counted")
        z0_ready, relu_done, y_ready, x1_ready = sem("z0_ready"), sem("relu_done"), sem("y_ready"), sem("x1_ready")
        t_ready, tc_done, sq_done, ss_done = sem("t_ready"), sem("tc_done"), sem("sq_done"), sem("ss_done")
        sd_done, rs_done, u_done = sem("sd_done"), sem("rs_done"), sem("u_done")
        hi_done, lo_done, turned, ut_ready = sem("hi_done"), sem("lo_done"), sem("turned"), sem("ut_ready")
        wide_ready, products, added = sem("wide_ready"), sem("products"), sem("added")
        leaky_done, spread, conv1_done, fin_ready = sem("leaky_done"), sem("spread"), sem("conv1_done"), sem("fin_ready")
        g_ready, h_ready, h1_ready, cf_raw = sem("g_ready"), sem("h_ready"), sem("h1_ready"), sem("cf_raw")
        cf_var, cf_sqrt, root_done = sem("cf_var"), sem("cf_sqrt"), sem("root_done")
        cf_step, cf_end, cf_made, last_two = sem("cf_step"), sem("cf_end"), sem("cf_made"), sem("last_two")

        block = ctx.enter_context(nc.Block())

        def sweep(eng, step, after_first=None, between=None):
            step(0, 0, 0, False)
            if after_first:
                after_first()
            step(0, 1, 1, False)
            with eng.Fori(2, UNITS) as m:
                step(0, m, 2, False)
            if between:
                between()
            with eng.Fori(1, PAIRS - 1) as n:
                with eng.Fori(0, UNITS) as m:
                    step(n, m, 2, False)
            with eng.Fori(0, UNITS - 1) as m:
                step(PAIRS - 1, m, 2, False)
            step(PAIRS - 1, UNITS - 1, 2, True)

        def pipeline(eng, begin, ahead, settle, start, turn, drain):
            begin()
            for t in range(4):
                ahead(t - t % 2, t % 2, t, True)
            with eng.Fori(2, LEAD // 2 - 1) as unit:
                for s in range(2):
                    ahead(unit * 2, s, 4, True)
            for s in range(2):
                ahead(LEAD - 2, s, 4, s == 0)
            settle()
            start()

            def turns(n, m, live, more, edge, last):
                for s in range(2):
                    turn(n, m, s, min(3, live + s), more, edge, not (last and s))

            END = UNITS - 1
            turns(0, 0, 0, True, False, False)
            turns(0, 1, 2, True, False, False)
            with eng.Fori(2, END) as m:
                turns(0, m, 3, True, False, False)
            turns(0, END, 3, True, True, False)
            with eng.Fori(1, PAIRS - 2) as n:
                with eng.Fori(0, END) as m:
                    turns(n, m, 3, True, False, False)
                turns(n, END, 3, True, True, False)
            with eng.Fori(0, END) as m:
                turns(PAIRS - 2, m, 3, True, False, False)
            turns(PAIRS - 2, END, 3, False, True, False)
            with eng.Fori(0, END) as m:
                turns(PAIRS - 1, m, 3, False, False, False)
            turns(PAIRS - 1, END, 3, False, False, True)
            drain()

        def chunk_before(t, s):
            return (t, 0) if s else (t - 2, 1)

        @block.sync
        def _(sp):
            for lo, hi in HALVES:
                sp.dma_start(wraw[lo:hi, :, :], w0.rearrange("o c a b -> c o (a b)")).then_inc(w_loaded, 16)
                sp.dma_start(par[lo:hi, 0:1], b0.rearrange("a c h w -> c (a h w)")).then_inc(b0_loaded, 16)

            def load_vectors():
                for lo, hi in HALVES:
                    for i, v in enumerate((gamma.rearrange("(c a) -> c a", a=1), beta.rearrange("(c a) -> c a", a=1),
                                           b1.rearrange("a c h w -> c (a h w)"),
                                           alpha.rearrange("(c a) -> c a", a=1),
                                           b2.rearrange("a c h w -> c (a h w)"),
                                           bias2.rearrange("(c a) -> c a", a=1))):
                        sp.dma_start(par[lo:hi, i + 1:i + 2], v).then_inc(par_loaded, 16)

            def load_x(n, m, before, last):
                for s in range(2):
                    for img, (lo, hi) in enumerate(HALVES):
                        if before:
                            sp.wait_ge(signed, n * (2 * CHUNKS) + m * 4 + (2 * s + img - 3))
                        sp.dma_start(xin[lo:hi, s], x_v[n, lo:hi, ds(m * 2 * ROWS + s * ROWS, ROWS), :])\
                            .then_inc(x_loaded[s][img], 16)

            sweep(sp, load_x, after_first=load_vectors)

            sp.wait_ge(signed, 2 * TOTAL)
            sp.wait_ge(counted, TOTAL)
            for s in range(2):
                sp.wait_ge(sums_stored[s], 16 * TOTAL // 2)

            def load(t, s, wait):
                if wait is not None:
                    sp.wait_ge(y_ready, wait)
                n, q = (t // CHUNKS, t % CHUNKS)
                sp.dma_start(xin[:, s], x_v[n, :, ds(q * ROWS, ROWS), :]).then_inc(in_loaded[s], 16)
                sp.dma_start(iin[:, s], sums[n, :, ds(q * ROWS, ROWS), :]).then_inc(in_loaded[s], 16)

            def store(t, s, done):
                sp.wait_ge(fin_ready, done * 2)
                n, q = (t // CHUNKS, t % CHUNKS)
                sp.dma_start(out_v[n, :, ds(q * ROWS, ROWS), :], fin[:, s]).then_inc(out_stored[s], 16)

            for s in range(2):
                load(s, s, None)
            FETCH = LEAD + 2
            with sp.Fori(1, FETCH // 2) as unit:
                for s in range(2):
                    load(unit * 2 + s, s, unit * 2 + (s - 1))
            for t in range(4):
                load(t + FETCH, t % 2, t + FETCH - 1)
                if t >= 3:
                    store(t - 3, (t - 3) % 2, t - 2)
            with sp.Fori(2, (TOTAL - FETCH) // 2) as unit:
                for s in range(2):
                    load(unit * 2 + (FETCH + s), s, unit * 2 + (FETCH + s - 1))
                    store(unit * 2 + (s - 3), 1 - s, unit * 2 + (s - 2))
            with sp.Fori((TOTAL - FETCH) // 2, TOTAL // 2 + 1) as unit:
                for s in range(2):
                    store(unit * 2 + (s - 3), 1 - s, unit * 2 + (s - 2))
            store(TOTAL - 1, 1, TOTAL)
            for s in range(2):
                sp.wait_ge(out_stored[s], 16 * TOTAL // 2)

        @block.gpsimd
        def _(pool):
            nc.gpsimd.memset(cw2t[:, :, :], 0.0).then_inc(pool_step, 1)
            pool.wait_ge(pool_step, 1)
            for i, (lo, hi) in enumerate(HALVES):
                for dst, src in ((w2raw[lo:hi, :, :], w2.rearrange("o c a k -> c o (a k)")),
                                 (wabs[lo:hi, :], w0.rearrange("o c a b -> o (c a b)")),
                                 (swraw[lo:hi, :], sw.rearrange("t c -> c t")),
                                 (cw1t[lo:hi, :], cw1.rearrange("m c -> c m")),
                                 (sbrow[0:1, i, :], sb.rearrange("(a t) -> a t", a=1)),
                                 (cw2t[0:MID, lo:hi, :].rearrange("m c k -> m (c k)"),
                                  cw2.rearrange("n m -> m n")),
                                 (cw2t[MID:MID + 1, lo:hi, :].rearrange("m c k -> m (c k)"),
                                  cb2.rearrange("(a n) -> a n", a=1))):
                    pool.dma_start(dst, src, allow_slow_non_contiguous=True).then_inc(aux_loaded, 16)
            pool.dma_start(cb1c[:, :], cb1.rearrange("(c a) -> c a", a=1), allow_slow_non_contiguous=True)\
                .then_inc(aux_loaded, 16)

            def constants():
                cleared = ((ident_f[:, :], 0.0), (sel_f[:, :, :], 0.0), (avg[:, :], 0.0), (g2[:, :], 0.0), (h1[:, :], 1.0),
                           (swbd[:, :], 0.0), (shift_wide[:, :], 1.0), (ones[:, :], 1.0))
                for t, v in cleared:
                    nc.gpsimd.memset(t, v).then_inc(pool_step, 1)
                step = 1 + len(cleared)
                pool.wait_ge(pool_step, step)
                chosen = [(ident_f[:, :], 1.0, 0, [[-1, 128]])]
                for part in range(PARTS):
                    for img in range(2):
                        chosen.append((sel_f[:, :, C * img:C * img + C], 1.0, -(SROW * part + TAPS * img),
                                       [[-1, TAPS], [0, C]]))
                for shift in (0, C, -C):
                    chosen.append((avg[:, :], 0.5, shift, [[-1, 128]]))
                for v, fill, base, pattern in chosen:
                    nc.gpsimd.affine_select(out=v, in_=v, compare_op=ALU.not_equal, fill=fill, base=base,
                                            pattern=pattern, channel_multiplier=1).then_inc(pool_step, 1)
                    step += 1
                    pool.wait_ge(pool_step, step)
                nc.gpsimd.memset(cft[:, :], 0.0).then_inc(const_made, 1)

            def store_sums(n, m, before, last):
                for s in range(2):
                    pool.wait_ge(upper_out, n * CHUNKS + m * 2 + (s + 1))
                    pool.wait_ge(lower_out, n * CHUNKS + m * 2 + (s + 1))
                    pool.dma_start(sums[n, :, ds(m * 2 * ROWS + s * ROWS, ROWS), :], iin[:, s])\
                        .then_inc(sums_stored[s], 16)

            sweep(pool, store_sums, after_first=constants)

            def norm_filter(t, s):
                pool.wait_ge(rs_done, t + (s + 1))
                o = u[:, (t + s) % USLOTS, :, :].rearrange("p r (a k) -> p r a k", a=2)
                nc.gpsimd.tensor_tensor(o, tc[:, s], trs[:, s].unsqueeze(3).broadcast_to([W, ROWS, 2, TAPS]),
                                        ALU.mult).then_inc(u_done, 1)

            def add_taps(n, m, s, live):
                t = n * CHUNKS + m * 2
                z_, ring = z[:, s], [prod[:, (TAPS * s + k) % RING] for k in range(TAPS)]
                for i, (dst, a, b, tap, earlier) in enumerate((
                        (z_, ring[0], ring[1], 1, None), (part[:, :, :], ring[2], ring[3], 3, 0),
                        (z_, z_, ring[4], 4, 1), (part[:, :, :], part[:, :, :], ring[5], 5, 2),
                        (z_, z_, ring[6], 6, 3), (part[:, :, :], part[:, :, :], ring[8], None, 4),
                        (z_, z_, part[:, :, :], None, 6))):
                    if i == 0 and live >= 2:
                        pool.wait_ge(spread, t + (s - 1))
                    if tap is not None:
                        pool.wait_ge(products, t * TAPS + (s * TAPS + tap + 1))
                    if i == 5:
                        pool.wait_ge(last_two, t + (s + 1))
                    if earlier or (earlier == 0 and live):
                        pool.wait_ge(added, t * ADDS + (s * ADDS + earlier))
                    nc.gpsimd.tensor_tensor(dst, a, b, ALU.add).then_inc(added, 1)

            def turn(n, m, s, live, more, edge, nxt):
                add_taps(n, m, s, live)
                if more:
                    norm_filter(n * CHUNKS + m * 2 + LEAD, s)

            def ahead(t, s, before, after):
                if before >= 2:
                    norm_filter(t - 2, s)

            def settle():
                for s in range(2):
                    norm_filter(LEAD - 2, s)

            pipeline(pool, lambda: None, ahead, settle, lambda: None, turn, lambda: None)

        @block.scalar
        def _(act):
            act.wait_ge(pads_zero, 1)
            nc.scalar.activation(cl["e4"], cl["e4"], ACT.Sqrt).then_inc(const_made, 1)
            act.wait_ge(pads_zero, 2)
            act.wait_ge(b0_loaded, 32)

            def upper_sums(t, s, stored):
                act.wait_ge(conv0_done, t * 2 + (2 * s + 1))
                if stored is not None:
                    act.wait_ge(counted, t + (s - 1))
                    act.wait_ge(sums_stored[s], stored)
                nc.scalar.activation(iin[:, s, 0:HR, :], wide[:, s, 0:HR, 0:W], ACT.Copy).then_inc(upper_out, 1)

            def sign_step(n, m, before, last):
                for s in range(2):
                    for img, (lo, hi) in enumerate(HALVES):
                        act.wait_ge(x_loaded[s][img], n * (16 * UNITS) + m * 16 + 16)
                        nc.scalar.activation(
                            signs[img][lo:hi, ds(m * 2 * ROWS + (s * ROWS + 1), ROWS), 1:W + 1], xin[lo:hi, s],
                            ACT.Sign, bias=par[lo:hi, 0:1]).then_inc(signed, 1)
                    if before:
                        upper_sums(n * CHUNKS + m * 2 - 2, s, n * (16 * UNITS) + m * 16 - 16 if before == 2 else None)

            def constants():
                act.wait_ge(const_made, 2)
                act.wait_ge(par_loaded, 16 * 2 * (NPAR - 1))
                nc.scalar.activation(ident[:, :], ident_f[:, :], ACT.Copy).then_inc(setup_ready, 1)
                nc.scalar.activation(sel[:, :, :], sel_f[:, :, :], ACT.Copy).then_inc(setup_ready, 1)

            sweep(act, sign_step, between=constants)
            for s in range(2):
                upper_sums(TOTAL - 2, s, 16 * (TOTAL // 2 - 1))

            def begin():
                act.wait_ge(bn_var, 1)
                nc.scalar.activation(cl["sd"], cl["ve"], ACT.Sqrt).then_inc(bn_sqrt, 1)
                act.wait_ge(bn_ready, 1)

            def negated(t, s, first):
                act.wait_ge(z0_ready, t + (s + 1))
                if not first:
                    act.wait_ge(t_ready, t + (s - 1))
                    act.wait_ge(x1_ready, t + (s - 1))
                nc.scalar.activation(y[:, s], xin[:, s], ACT.Relu, bias=cl["nB"], scale=-1.0).then_inc(relu_done, 1)

            def keep_x1(t, s):
                act.wait_ge(y_ready, t + (s + 1))
                pair, q = (t + s) // CHUNKS, (t + s) % CHUNKS
                nc.scalar.activation(x1[:, pair % 2, ds(q * ROWS + 1, ROWS), 1:W + 1], y[:, s], ACT.Identity,
                                     bias=cl["shift"],
                                     accum_out=gs[:, pair % 2, ds(q, 1)]).then_inc(x1_ready, 1)

            def square(t, s):
                act.wait_ge(tc_done, t + (s + 1))
                nc.scalar.activation(tsq[:, :, :, :], tc[:, s], ACT.Square).then_inc(sq_done, 1)

            def root(t, s):
                act.wait_ge(ss_done, t + (s + 1))
                nc.scalar.activation(tsd[:, s], tss[:, s], ACT.Sqrt, scale=1.0 / (TAPS - 1)).then_inc(root_done, 1)
                act.wait_ge(root_done, t + (s + 1))
                nc.scalar.activation(tsd[:, s], tsd[:, s], ACT.Identity, bias=cl["tiny"][0:W, :]).then_inc(sd_done, 1)

            def ahead(t, s, before, after):
                negated(t, s, before < 2)
                if before >= 1:
                    keep_x1(*chunk_before(t, s))
                if before >= 2:
                    square(t - 2, s)
                    root(t - 2, s)

            def settle():
                keep_x1(LEAD - 2, 1)
                for s in range(2):
                    square(LEAD - 2, s)
                    root(LEAD - 2, s)

            def high_part(t, o, s, reuse):
                act.wait_ge(u_done, t + (o + 1))
                if reuse:
                    act.wait_ge(turned, t * 2 + 2 * (o - 1))
                nc.scalar.activation(us[:, s, :, 0:SROW], u[:, (t + o) % USLOTS, :, :], ACT.Copy).then_inc(hi_done, 1)

            def take_turned(t, o, s, h):
                act.wait_ge(turned, t * 2 + (2 * o + h + 1))
                nc.scalar.activation(ut[0:UROW, s, HR * h:HR * h + HR, :],
                                     pu[0:UROW, 0:HR * W].rearrange("p (r w) -> p r w", r=HR), ACT.Copy)\
                    .then_inc(ut_ready, 1)

            def spread_rows(t, o, s, half, reuse):
                if half == 0:
                    act.wait_ge(leaky_done, t + (o + 1))
                    if reuse:
                        act.wait_ge(conv1_done, t * 2 + 2 * (o - 1))
                a, b = (0, 64), (64, 128)
                dst, d, at, src = ((xa, a, FPAD, a), (xa, b, FPAD - 1, a), (xb, b, FPAD, b), (xb, a, FPAD - 1, b))[half]
                i = nc.scalar.activation(dst[d[0]:d[1], s, :, at:at + W], z[src[0]:src[1], s], ACT.Copy)
                if half == 3:
                    i.then_inc(spread, 1)

            def finish(t, o, s, h, reuse):
                act.wait_ge(conv1_done, t * 2 + (2 * o + h + 1))
                if h == 0 and reuse:
                    act.wait_ge(out_stored[s], t * 8 + (16 * ((o - 2 - s) // 2) + 16))
                nc.scalar.activation(fin[:, s, HR * h:HR * h + HR, :], acc[:, HR * h:HR * h + HR, 0:W], ACT.Identity,
                                     bias=P_BIAS2).then_inc(fin_ready, 1)

            def hidden(pair):
                act.wait_ge(h_ready, pair + 1)
                nc.scalar.activation(h1[0:MID, :], pt[0:MID, 0:2], ACT.Relu, bias=cb1c[:, :], scale=1.0 / (H * W))\
                    .then_inc(h1_ready, 1)

            def cf_root(pair):
                act.wait_ge(cf_var, pair + 1)
                nc.scalar.activation(cft[:, 2:3], cft[:, 1:2], ACT.Sqrt, scale=1.0 / (TAPS - 1)).then_inc(cf_sqrt, 1)

            def turn(n, m, s, live, more, edge, nxt):
                t = n * CHUNKS + m * 2
                if nxt:
                    high_part(t, s + 1, 1 - s, live >= 1)
                if live >= 3:
                    finish(t, s - 3, 1 - s, 1, True)
                if more:
                    negated(t + LEAD, s, False)
                    keep_x1(t + LEAD, s)
                if nxt:
                    take_turned(t, s + 1, 1 - s, 0)
                    take_turned(t, s + 1, 1 - s, 1)
                if live >= 2:
                    finish(t, s - 2, s, 0, not (isinstance(n, int) and n == 0 and isinstance(m, int) and m < 2))
                if edge and s == 1:
                    cf_root(n + 1)
                for half in range(4):
                    if live >= 1:
                        spread_rows(t, s - 1, 1 - s, half, live >= 3)
                if more:
                    square(t + LEAD, s)
                    root(t + LEAD, s)
                if edge and s == 0:
                    hidden(n + 1)

            def start():
                hidden(0)
                cf_root(0)
                high_part(0, 0, 0, False)
                take_turned(0, 0, 0, 0)
                take_turned(0, 0, 0, 1)

            def drain():
                finish(TOTAL, -3, 1, 1, True)
                for half in range(4):
                    spread_rows(TOTAL, -1, 1, half, True)
                for h in range(2):
                    finish(TOTAL, -2, 0, h, True)
                for h in range(2):
                    finish(TOTAL, -1, 1, h, True)

            pipeline(act, begin, ahead, settle, start, turn, drain)

        @block.vector
        def _(dve):
            links = [0]

            def link(i):
                links[0] += 1
                i.then_inc(chain, 1)
                dve.wait_ge(chain, links[0])

            link(nc.vector.memset(col[:, :], 0.0))
            nc.vector.memset(cl["tiny"], 1e-10).then_inc(pads_zero, 1)
            for image in signs:
                nc.vector.memset(image[:, 0:1, :], 0.0)
                nc.vector.memset(image[:, HP - 1:HP, :], 0.0)
                nc.vector.memset(image[:, 1:HP - 1, 0:1], 0.0)
                i = nc.vector.memset(image[:, 1:HP - 1, WP - 2:WP], 0.0)
            i.then_inc(pads_zero, 1)
            nc.vector.memset(us[:, :, :, :].bitcast(fp32), 0.0)
            nc.vector.memset(ut[:, :, :, :].bitcast(fp32), 0.0)
            link(nc.vector.memset(wbin[:, :, :, :], 0.0))
            dve.wait_ge(w_loaded, 32)
            link(nc.vector.tensor_scalar(wraw[:, :, :], wraw[:, :, :], 0.0, 2.0, ALU.is_gt, ALU.mult))
            for img, (lo, hi) in enumerate(HALVES):
                olo, ohi = HALVES[1 - img]
                for a, b, at, tap in ((lo, hi, 0, 0), (olo, ohi, 0, 1), (lo, hi, K, 2)):
                    nc.vector.tensor_scalar(wbin[a:b, img, at:at + K, :],
                                            wraw[a:b, :, tap:TAPS:K].rearrange("c o k -> c k o"), -1.0, None, ALU.add)\
                        .then_inc(wbin_ready, 1)

            def lower_sums(t, s, stored):
                dve.wait_ge(conv0_done, t * 2 + (2 * s + 2))
                if stored is not None:
                    dve.wait_ge(sums_stored[s], stored)
                nc.vector.tensor_copy(iin[:, s, HR:ROWS, :], wide[:, s, HR:ROWS, 0:W]).then_inc(lower_out, 1)
                for h, out_of in ((0, upper_out), (1, lower_out)):
                    dve.wait_ge(out_of, t + (s + 1))
                    i = nc.vector.bn_stats(stats[:, ds(t * 2 + (2 * s + h), 1), :].rearrange("p a s -> p (a s)"),
                                           iin[:, s, HR * h:HR * h + HR, :])
                i.then_inc(counted, 1)

            def shift_step(n, m, before, last):
                for s in range(2):
                    for img, (lo, hi) in enumerate(HALVES):
                        dve.wait_ge(signed, n * (2 * CHUNKS) + m * 4 + (2 * s + img + 1))
                        olo, ohi = HALVES[1 - img]
                        rows = ds(m * 2 * ROWS + (s * ROWS + 1), ROWS)
                        i = nc.vector.tensor_copy(signs[img][olo:ohi, rows, 0:W],
                                                  signs[img][lo:hi, rows, 1:W + 1])
                    i.then_inc(shifted, 1)
                    if before:
                        lower_sums(n * CHUNKS + m * 2 - 2, s, n * (16 * UNITS) + m * 16 - 16 if before == 2 else None)

            def constants():
                dve.wait_ge(const_made, 2)
                dve.wait_ge(aux_loaded, 16 * (2 * 7 + 1))
                dve.wait_ge(par_loaded, 16 * 2 * (NPAR - 1))
                link(nc.vector.scalar_tensor_tensor(wabs[:, :], wabs[:, :], -1.0, wabs[:, :], ALU.mult, ALU.max))
                link(nc.vector.tensor_reduce(cl["wsum"], wabs[:, :], AX.X, ALU.add))
                link(nc.vector.tensor_scalar(cl["scale"], cl["wsum"], 1.0 / (C * TAPS), None, ALU.mult))
                link(nc.vector.tensor_reduce(cl["cs"], swraw[:, :], AX.X, ALU.add))
                link(nc.vector.tensor_scalar(cl["negm"], cl["cs"], -1.0 / TAPS, None, ALU.mult))
                for i, (lo, hi) in enumerate(HALVES):
                    link(nc.vector.tensor_scalar(swbd[lo:hi, TAPS * i:TAPS * i + TAPS], swraw[lo:hi, :],
                                                 cl["negm"][lo:hi, :], None, ALU.add))
                link(nc.vector.tensor_reduce(sbc[0:1, 0, 0:1], sbrow[0:1, 0, :], AX.X, ALU.add))
                link(nc.vector.tensor_scalar(sbc[0:1, 0, 1:2], sbc[0:1, 0, 0:1], -1.0 / TAPS, None, ALU.mult))
                link(nc.vector.tensor_scalar(sbrow[0:1, :, :], sbrow[0:1, :, :], sbc[0:1, 0, 1:2], None, ALU.add))
                link(nc.vector.tensor_scalar(cl["rise"], P_ALPHA, -1.0, 1.0, ALU.mult, ALU.add))
                for lo, hi in HALVES:
                    img = lo // C
                    olo, ohi = C - lo, 2 * C - lo
                    link(nc.vector.tensor_copy(w2t[lo:hi, img, :, :], w2raw[lo:hi, :, 0:FW:2].rearrange("c o k -> c k o")))
                    link(nc.vector.tensor_copy(w2t[olo:ohi, img, 0:FP - 1, :],
                                               w2raw[olo:ohi, :, 1:FW:2].rearrange("c o k -> c k o")))
                nc.vector.tensor_copy(cl["e4"], cl["negm"]).then_inc(setup_ready, 1)

            def clear():
                for t in (xa, xb, w2t):
                    i = nc.vector.memset(t[:, :, :, :], 0.0)
                link(i)

            sweep(dve, shift_step, after_first=clear, between=constants)
            for s in range(2):
                lower_sums(TOTAL - 2, s, 16 * (TOTAL // 2 - 1))

            def begin():
                dve.wait_ge(counted, TOTAL)
                link(nc.vector.bn_aggr(col[:, 2:4], stats[:, 0:2 * TOTAL, :]))
                nc.vector.memset(x1[:, :, 0:1, :], 0.0)
                nc.vector.memset(x1[:, :, HP - 1:HP, :], 0.0)
                nc.vector.memset(x1[:, :, 1:HP - 1, 0:1], 0.0)
                link(nc.vector.memset(x1[:, :, 1:HP - 1, WP - 1:WP], 0.0))
                nc.vector.tensor_scalar(cl["e4"], cl["mean"], 1.0, None, ALU.mult).then_inc(agg_ready, 1)
                dve.wait_ge(avg_ready, 1)
                link(nc.vector.tensor_copy(col[:, 4:6], pt[:, 0:2]))
                link(nc.vector.tensor_tensor(cl["d"], cl["mean"], cl["gmean"], ALU.subtract))
                link(nc.vector.tensor_tensor(cl["d2"], cl["d"], cl["d"], ALU.mult))
                link(nc.vector.tensor_tensor(cl["v"], cl["gvar"], cl["d2"], ALU.add))
                link(nc.vector.tensor_tensor(cl["sv"], cl["v"], cl["scale"], ALU.mult))
                link(nc.vector.tensor_scalar(cl["ve"], cl["sv"], cl["scale"], BN_EPS, ALU.mult, ALU.add))
                nc.vector.tensor_copy(cl["e1"], cl["ve"]).then_inc(bn_var, 1)
                dve.wait_ge(bn_sqrt, 1)
                link(nc.vector.reciprocal(cl["r"], cl["sd"]))
                link(nc.vector.tensor_tensor(cl["e2"], cl["r"], cl["r"], ALU.mult))
                link(nc.vector.tensor_tensor(cl["e3"], cl["e2"], cl["ve"], ALU.mult))
                link(nc.vector.tensor_scalar(cl["e2"], cl["e3"], -0.5, 1.5, ALU.mult, ALU.add))
                link(nc.vector.tensor_tensor(cl["e3"], cl["e2"], cl["r"], ALU.mult))
                link(nc.vector.tensor_tensor(cl["e2"], cl["e3"], cl["scale"], ALU.mult))
                link(nc.vector.tensor_tensor(cl["A"], cl["e2"], P_GAMMA, ALU.mult))
                link(nc.vector.tensor_tensor(cl["mA"], cl["gmean"], cl["A"], ALU.mult))
                link(nc.vector.tensor_tensor(cl["e3"], P_BETA, cl["mA"], ALU.subtract))
                link(nc.vector.tensor_tensor(cl["Bc"], cl["e3"], P_B1, ALU.add))
                link(nc.vector.tensor_scalar(cl["nB"], cl["Bc"], -1.0, None, ALU.mult))
                link(nc.vector.tensor_tensor(cl["shift"], cl["Bc"], P_B2, ALU.add))
                nc.vector.tensor_copy(cl["e2"], cl["nB"]).then_inc(bn_ready, 1)
                nc.vector.tensor_scalar(shift_wide[:, :], shift_wide[:, :], cl["shift"], None, ALU.mult).then_inc(setup_ready, 1)
                dve.wait_ge(tb_ready, 1)
                nc.vector.tensor_copy(tbias[:, :, :], pt[0:W, 0:SROW].rearrange("p (a k) -> p a k", a=2))

            def add_residual(t, s):
                dve.wait_ge(in_loaded[s], t * 16 + 32)
                nc.vector.scalar_tensor_tensor(xin[:, s], iin[:, s], cl["A"], xin[:, s], ALU.mult, ALU.add)\
                    .then_inc(z0_ready, 1)

            def prelu(t, s):
                dve.wait_ge(relu_done, t + (s + 1))
                nc.vector.scalar_tensor_tensor(y[:, s], y[:, s], cl["rise"], xin[:, s], ALU.mult, ALU.add)\
                    .then_inc(y_ready, 1)

            def centre(t, s, first):
                dve.wait_ge(t_ready, t + (s + 1))
                if not first:
                    dve.wait_ge(u_done, t + (s - 1))
                nc.vector.tensor_tensor(tc[:, s], pt_v, tbias[:, :, :].unsqueeze(1).broadcast_to([W, ROWS, 2, TAPS]),
                                        ALU.add).then_inc(tc_done, 1)

            def sum_squares(t, s):
                dve.wait_ge(sq_done, t + (s + 1))
                nc.vector.tensor_reduce(tss[:, s], tsq[:, :, :, :], AX.X, ALU.add).then_inc(ss_done, 1)

            def inverse(t, s):
                dve.wait_ge(sd_done, t + (s + 1))
                nc.vector.reciprocal(trs[:, s], tsd[:, s]).then_inc(rs_done, 1)

            def ahead(t, s, before, after):
                if before == 0:
                    add_residual(t, s)
                prelu(t, s)
                if after:
                    if s == 0:
                        add_residual(t, 1)
                    else:
                        add_residual(t + 2, 0)
                if before >= 2:
                    sum_squares(t - 2, s)
                    inverse(t - 2, s)
                if before >= 1:
                    centre(*chunk_before(t, s), before < 3)

            def settle():
                sum_squares(LEAD - 2, 0)
                inverse(LEAD - 2, 0)
                centre(LEAD - 2, 1, False)
                sum_squares(LEAD - 2, 1)
                inverse(LEAD - 2, 1)

            def low_part(t, o, s):
                dve.wait_ge(hi_done, t + (o + 1))
                nc.vector.tensor_tensor(us[:, s, :, SROW:UROW], u[:, (t + o) % USLOTS, :, :],
                                        us[:, s, :, 0:SROW].bitcast(fp32), ALU.subtract).then_inc(lo_done, 1)

            USED_BY = {0: 2, 1: 3, 2: 4, 3: 5, 5: 6, 6: 1, 7: 1, 8: 2}

            def product(n, m, s, k, live):
                t = n * CHUNKS + m * 2
                if k == 0:
                    dve.wait_ge(cf_made, n + 1)
                if k == 4 and live:
                    dve.wait_ge(last_two, t + s)
                elif k != 4 and (live or k >= RING):
                    dve.wait_ge(added, t * ADDS + (ADDS * (s if k >= RING else s - 1) + USED_BY[k]))
                dve.wait_ge(wide_ready, t * TAPS + (s * TAPS + k + 1))
                nc.vector.scalar_tensor_tensor(
                    prod[:, (TAPS * s + k) % RING],
                    x1[:, n % 2, ds(m * 2 * ROWS + (s * ROWS + k // K), ROWS), k % K:k % K + W],
                    cfn[:, k:k + 1], wide[:, (TAPS * s + k) % 2, :, 0:W], ALU.mult, ALU.mult).then_inc(products, 1)

            def add_last_two(n, m, s):
                t = n * CHUNKS + m * 2
                a, b = (TAPS * s + TAPS - 2) % RING, (TAPS * s + TAPS - 1) % RING
                dve.wait_ge(products, t * TAPS + (s + 1) * TAPS)
                nc.vector.tensor_tensor(prod[:, b], prod[:, a], prod[:, b], ALU.add).then_inc(last_two, 1)

            def leaky(t, o, s):
                dve.wait_ge(added, t * ADDS + ADDS * (o + 1))
                nc.vector.scalar_tensor_tensor(z[:, s], z[:, s], 0.1, z[:, s], ALU.mult, ALU.max)\
                    .then_inc(leaky_done, 1)

            def sum_images(pair):
                dve.wait_ge(x1_ready, pair * CHUNKS + CHUNKS)
                nc.vector.tensor_reduce(cft[:, 0:1], gs[:, pair % 2, :], AX.X, ALU.add).then_inc(cf_step, 1)

            def place_sums(pair):
                dve.wait_ge(cf_step, pair * 6 + 1)
                for i, (lo, hi) in enumerate(HALVES):
                    nc.vector.tensor_copy(g2[lo:hi, i:i + 1], cft[lo:hi, 0:1]).then_inc(g_ready, 1)

            def cf_centre(pair):
                dve.wait_ge(cf_raw, pair + 1)
                cfp = pt[:, 64:64 + 2 * TAPS].rearrange("p (k i) -> p k i", i=2)
                for i, (lo, hi) in enumerate(HALVES):
                    nc.vector.tensor_copy(cf[lo:hi, :], cfp[lo:hi, :, i]).then_inc(cf_step, 1)
                dve.wait_ge(cf_step, pair * 6 + 3)
                nc.vector.tensor_reduce(cft[:, 0:1], cf[:, :], AX.X, ALU.add).then_inc(cf_step, 1)
                dve.wait_ge(cf_step, pair * 6 + 4)
                nc.vector.tensor_scalar(cft[:, 3:4], cft[:, 0:1], -1.0 / TAPS, None, ALU.mult).then_inc(cf_step, 1)
                dve.wait_ge(cf_step, pair * 6 + 5)
                nc.vector.tensor_scalar(cfc[:, :], cf[:, :], cft[:, 3:4], None, ALU.add).then_inc(cf_step, 1)

            def cf_squares(pair):
                dve.wait_ge(cf_step, pair * 6 + 6)
                nc.vector.tensor_tensor(cfq[:, :], cfc[:, :], cfc[:, :], ALU.mult).then_inc(cf_end, 1)
                dve.wait_ge(cf_end, pair * 3 + 1)
                nc.vector.tensor_reduce(cft[:, 1:2], cfq[:, :], AX.X, ALU.add).then_inc(cf_var, 1)

            def cf_scale(pair):
                dve.wait_ge(cf_sqrt, pair + 1)
                nc.vector.tensor_scalar(cft[:, 0:1], cft[:, 2:3], 1e-10, None, ALU.add).then_inc(cf_end, 1)
                dve.wait_ge(cf_end, pair * 3 + 2)
                nc.vector.reciprocal(cft[:, 3:4], cft[:, 0:1]).then_inc(cf_end, 1)

            def cf_finish(pair):
                dve.wait_ge(cf_end, pair * 3 + 3)
                nc.vector.tensor_scalar(cfn[:, :], cfc[:, :], cft[:, 3:4], STD2, ALU.mult, ALU.mult)\
                    .then_inc(cf_made, 1)

            def start():
                for step in (sum_images, place_sums, cf_centre, cf_squares, cf_scale, cf_finish):
                    step(0)
                low_part(0, 0, 0)

            def turn(n, m, s, live, more, edge, nxt):
                t = n * CHUNKS + m * 2
                if more:
                    add_residual(t + LEAD, s)
                product(n, m, s, 0, live)
                if edge and s == 0:
                    sum_images(n + 1)
                product(n, m, s, 1, live)
                if edge and s == 0:
                    place_sums(n + 1)
                if nxt:
                    low_part(t, s + 1, 1 - s)
                if more:
                    prelu(t + LEAD, s)
                if edge and s == 1:
                    cf_centre(n + 1)
                product(n, m, s, 2, live)
                product(n, m, s, 3, live)
                if edge and s == 1:
                    cf_squares(n + 1)
                product(n, m, s, 4, live)
                if live >= 1:
                    leaky(t, s - 1, 1 - s)
                product(n, m, s, 5, live)
                product(n, m, s, 6, live)
                if more:
                    centre(t + LEAD, s, False)
                product(n, m, s, 7, live)
                if more:
                    sum_squares(t + LEAD, s)
                if edge and s == 1:
                    cf_scale(n + 1)
                product(n, m, s, 8, live)
                if more:
                    inverse(t + LEAD, s)
                add_last_two(n, m, s)
                if edge and s == 1:
                    cf_finish(n + 1)

            def drain():
                leaky(TOTAL, -1, 1)

            pipeline(dve, begin, ahead, settle, start, turn, drain)

        @block.tensor
        def _(pe):
            pe.wait_ge(wbin_ready, 6)

            def conv0_pair(n, first):
                for q in range(CHUNKS):
                    t, s = n * CHUNKS, q % 2
                    pe.wait_ge(shifted, t + min(q + 2, CHUNKS))
                    for h, out_of in ((0, upper_out), (1, lower_out)):
                        if not first or q >= 2:
                            pe.wait_ge(out_of, t + (q - 1))
                        for k in range(2 * K):
                            for img in range(2):
                                row, column = q * ROWS + HR * h + k % K, 2 * (k // K)
                                i = nc.tensor.matmul(
                                    wide[C * img:C * img + C, s, HR * h:HR * h + HR, 0:W], wbin[:, img, k, :],
                                    signs[img][:, row:row + HR, column:column + W],
                                    start=k == 0, stop=k == 2 * K - 1)
                        i.then_inc(conv0_done, 1)

            conv0_pair(0, True)
            with pe.Fori(1, PAIRS) as n:
                conv0_pair(n, False)

            def begin():
                pe.wait_ge(setup_ready, 3)
                pe.wait_ge(agg_ready, 1)
                nc.tensor.matmul(pt[:, 0:2], avg[:, :], col[:, 2:4], start=True, stop=True).then_inc(avg_ready, 1)
                pe.wait_ge(setup_ready, 4)
                nc.tensor.matmul(pt[0:W, 0:SROW], shift_wide[:, :], swbd[:, :], start=True, stop=False)
                nc.tensor.matmul(pt[0:W, 0:SROW], ones[:, :], sbrow[0:1, :, :].rearrange("p a k -> p (a k)"),
                                 start=False, stop=True).then_inc(tb_ready, 1)
                pe.wait_ge(upper_out, TOTAL)
                pe.wait_ge(lower_out, TOTAL)

            def spatial(t, s, before, after):
                pe.wait_ge(y_ready, t + (s + 1))
                if before:
                    pe.wait_ge(tc_done, t + s)
                spatial_rows(s, 0, ROWS)

            def spatial_rows(s, a, b):
                for r in range(a, b):
                    i = nc.tensor.matmul(pt[0:W, SROW * r:SROW * r + SROW], y[:, s, r, :], swbd[:, :],
                                         start=True, stop=True)
                if b == ROWS:
                    i.then_inc(t_ready, 1)

            def turn_back(t, o, s, h, first):
                if h == 0:
                    pe.wait_ge(lo_done, t + (o + 1))
                if not (first and h == 0):
                    pe.wait_ge(ut_ready, t * 2 + (2 * o + h))
                for r in range(HR):
                    i = nc.tensor.matmul(pu[0:UPAD, W * r:W * r + W], us[:, s, HR * h + r, :], ident[0:W, 0:W],
                                         start=True, stop=True)
                i.then_inc(turned, 1)

            def spread_tap(n, m, s, k, live):
                p = (n * CHUNKS + m * 2) * TAPS
                if k == 0:
                    pe.wait_ge(ut_ready, (n * CHUNKS + m * 2) * 2 + (2 * s + 2))
                if live or k >= 2:
                    pe.wait_ge(products, p + (s * TAPS + k - 1))
                for h in range(2):
                    i = nc.tensor.matmul(wide[:, (TAPS * s + k) % 2, HR * h:HR * h + HR, 0:W], sel[:, k, :],
                                         ut[:, s, HR * h:HR * h + HR, :], start=True, stop=True)
                i.then_inc(wide_ready, 1)

            def conv1(t, o, s, a, b, reuse):
                c = t + o
                for j in range(a, b):
                    h, i = j // BANK1, j % BANK1
                    if j == 0:
                        pe.wait_ge(spread, t + (o + 1))
                    if i == 0:
                        if reuse:
                            pe.wait_ge(fin_ready, t * 2 + (2 * o + h - 1))
                        nc.tensor.matmul(
                            acc[:, HR * h:HR * h + HR, 0:W], ident[:, :].bitcast(fp32),
                            x1[:, (c // CHUNKS) % 2, ds((c % CHUNKS) * ROWS + (HR * h + 1), HR), 1:W + 1],
                            start=True, stop=False)
                        continue
                    p, img = (i - 1) // 2, (i - 1) % 2
                    src = (xa, xb)[img]
                    mm = nc.tensor.matmul(acc[C * img:C * img + C, HR * h:HR * h + HR, 0:W], w2t[:, img, p, :],
                                          src[:, s, HR * h:HR * h + HR, 2 * p:2 * p + W],
                                          start=False, stop=p == FP - 1)
                    if i == BANK1 - 1:
                        mm.then_inc(conv1_done, 1)

            BANK1 = 2 * FP + 1
            cuts = [0, 4, 8, 11, 12, 14, 15, 17, 19, 22]

            def hidden(pair):
                pe.wait_ge(g_ready, pair * 2 + 2)
                nc.tensor.matmul(pt[0:MID, 0:2], cw1t[:, :], g2[:, :], start=True, stop=True).then_inc(h_ready, 1)

            def channel(pair):
                pe.wait_ge(h1_ready, pair + 1)
                for k in range(TAPS):
                    i = nc.tensor.matmul(pt[:, 64 + 2 * k:66 + 2 * k], cw2t[:, :, k], h1[:, :], start=True, stop=True)
                i.then_inc(cf_raw, 1)

            def turn(n, m, s, live, more, edge, nxt):
                t = n * CHUNKS + m * 2
                for k in range(TAPS):
                    spread_tap(n, m, s, k, live)
                    if k == 1 and edge and s == 1:
                        channel(n + 1)
                    if k == 3 and more:
                        if edge and s == 1:
                            pe.wait_ge(cf_step, n * 6 + 9)
                        pe.wait_ge(y_ready, t + (LEAD + s + 1))
                        pe.wait_ge(tc_done, t + (LEAD + s))
                    if 3 <= k < 7 and more:
                        spatial_rows(s, 2 * k - 6, 2 * k - 4)
                    if k == 8 and edge and s == 0:
                        if more:
                            pe.wait_ge(tc_done, t + (LEAD + 1))
                        hidden(n + 1)
                    if live >= 2:
                        conv1(t, s - 2, s, cuts[k], cuts[k + 1], live >= 3)
                    if k == 2 and nxt:
                        turn_back(t, s + 1, 1 - s, 0, False)
                    if k == 4 and nxt:
                        turn_back(t, s + 1, 1 - s, 1, False)

            def start():
                pe.wait_ge(tc_done, LEAD)
                hidden(0)
                channel(0)
                turn_back(0, 0, 0, 0, True)
                turn_back(0, 0, 0, 1, True)
                pe.wait_ge(cf_var, 1)

            def drain():
                conv1(TOTAL, -2, 0, 0, 2 * BANK1, True)
                conv1(TOTAL, -1, 1, 0, 2 * BANK1, True)

            pipeline(pe, begin, spatial, lambda: None, start, turn, drain)


_INS = ["x", "L0_conv_b0", "L0_conv_w", "L0_conv_gamma", "L0_conv_beta", "L0_conv_b1", "L0_conv_alpha", "L0_conv_b2",
        "L1_conv_sw", "L1_conv_sb", "L1_conv_cw1", "L1_conv_cb1", "L1_conv_cw2", "L1_conv_cb2", "L1_conv_w2",
        "L1_conv_b2"]


def kernel(**inputs):
    import numpy as _np
    import concourse.bacc as _bacc
    from concourse import mybir as _mybir
    from concourse.bass_utils import run_bass_kernel_spmd as _run

    nc = _bacc.Bacc("TRN2", target_bir_lowering=False, num_devices=1)
    arrays, args = {}, []
    for name in _INS:
        a = _np.ascontiguousarray(inputs[name])
        arrays[f"in_{name}"] = a
        args.append(nc.dram_tensor(f"in_{name}", a.shape, _mybir.dt.from_np(a.dtype), kind="ExternalInput").ap())
    out = nc.dram_tensor("out", inputs["x"].shape, _mybir.dt.float32, kind="ExternalOutput").ap()
    build(nc, *args, out)
    r = _run(nc, [arrays], core_ids=[0])
    return r.results[0]["out"]
```
